# Optimizing a Trainium2 kernel written in Bass

```python
import numpy as np
import jax
import jax.numpy as jnp

def _softmax(x, axis=-1):
    return jax.nn.softmax(x, axis=axis)

def _gelu(x):
    return jax.nn.gelu(x, approximate=True)

def _silu(x):
    return jax.nn.silu(x)

def _sigmoid(x):
    return jax.nn.sigmoid(x)

def _layernorm(x, axis=-1, eps=1e-05):
    m = jnp.mean(x, axis=axis, keepdims=True)
    v = jnp.var(x, axis=axis, keepdims=True)
    return (x - m) / jnp.sqrt(v + eps)

def _scatter_add(tgt, idx, src, axis=0):
    return tgt.at[idx].add(src)

def _segment_sum(src, seg, n):
    return jax.ops.segment_sum(src, seg, n)
kernel_name = 'mk_perceiver_d1_seqx_r4_0aa1ea'

def setup_inputs(seed: int=0):
    np.random.seed(seed)
    _w = jnp.asarray

    def _rec_inputs():
        import jax
        import jax.numpy as jnp
        _rk = jax.random.key(seed)
        x = -0.0002928 + 1 * jax.random.normal(jax.random.fold_in(_rk, 1), (128, 32, 256), jnp.float32)
        _lenS = 32 - jax.random.randint(jax.random.fold_in(_rk, 7), (128,), 0, max(1, 32 // 4) + 1, jnp.int32)
        _lenS2 = 257 - jax.random.randint(jax.random.fold_in(_rk, 8), (128,), 0, max(1, 257 // 4) + 1, jnp.int32)
        _ctx_1024P = jax.random.normal(jax.random.fold_in(_rk, 11), (128, 16, 256), jnp.float32)
        _ctx_1024c = jax.random.dirichlet(jax.random.fold_in(_rk, 511), 0.3 * jnp.ones((16,), jnp.float32), (128, 257))
        _ctx_1024t = jnp.einsum('bsk,bkd->bsd', _ctx_1024c, _ctx_1024P)
        _ctx_1024t = _ctx_1024t * jax.lax.rsqrt(jnp.mean(jnp.square(_ctx_1024t)) + 1e-12) * 0.953939
        ctx_1024 = -1.39393e-06 + 0.999914 * (_ctx_1024t + 0.3 * jax.random.normal(jax.random.fold_in(_rk, 611), (128, 257, 256), jnp.float32))
        return (x, ctx_1024)
    x, ctx_1024 = _rec_inputs()

    def _L0_xattn_setup():
        import jax, jax.numpy as jnp
        import numpy as np
        DIM = 256
        HEADS = 16
        HEAD_DIM = DIM // HEADS
        SCALE = HEAD_DIM ** (-0.5)
        key = jax.random.key(seed)
        ks = jax.random.split(key, 7)
        b, n = (2, 512)
        x1 = jax.random.normal(ks[0], (b, n, DIM), dtype=jnp.float32)
        x2 = jax.random.normal(ks[1], (b, n, DIM), dtype=jnp.float32)
        s = DIM ** (-0.5)
        wq = jax.random.normal(ks[2], (DIM, DIM), dtype=jnp.float32) * s
        wk = jax.random.normal(ks[3], (DIM, DIM), dtype=jnp.float32) * s
        wv = jax.random.normal(ks[4], (DIM, DIM), dtype=jnp.float32) * s
        wo = jax.random.normal(ks[5], (DIM, DIM), dtype=jnp.float32) * s
        bo = jax.random.normal(ks[6], (DIM,), dtype=jnp.float32) * 0.01
        return {'x1': x1, 'x2': x2, 'wq': wq, 'wk': wk, 'wv': wv, 'wo': wo, 'bo': bo}
    _L0_xattn_all = _L0_xattn_setup()
    _L0_xattn_in = {k: v for k, v in _L0_xattn_all.items() if k in ('wq', 'wk', 'wv', 'wo', 'bo')}
    del _L0_xattn_all

    def _L0_attn_setup():
        import jax, jax.numpy as jnp
        import numpy as np
        D_MODEL = 256
        N_HEADS = 16
        D_HEAD = D_MODEL // N_HEADS
        EPS = 1e-06
        B, N = (1, 512)

        def _phi(x):
            return jax.nn.elu(x) + 1.0

        def _split_heads(y, b, n):
            return y.reshape(b, n, N_HEADS, D_HEAD).transpose(0, 2, 1, 3)
        key = jax.random.key(seed)
        ks = jax.random.split(key, 10)
        s = 1.0 / np.sqrt(D_MODEL)
        return {'x': jax.random.normal(ks[0], (B, N, D_MODEL), dtype=jnp.float32), 'mask': jnp.tril(jnp.ones((N, N), dtype=bool)), 'Wq': jax.random.normal(ks[1], (D_MODEL, D_MODEL), dtype=jnp.float32) * s, 'bq': jax.random.normal(ks[2], (D_MODEL,), dtype=jnp.float32) * s, 'Wk': jax.random.normal(ks[3], (D_MODEL, D_MODEL), dtype=jnp.float32) * s, 'bk': jax.random.normal(ks[4], (D_MODEL,), dtype=jnp.float32) * s, 'Wv': jax.random.normal(ks[5], (D_MODEL, D_MODEL), dtype=jnp.float32) * s, 'bv': jax.random.normal(ks[6], (D_MODEL,), dtype=jnp.float32) * s, 'Wo': jax.random.normal(ks[7], (D_MODEL, D_MODEL), dtype=jnp.float32) * s, 'bo': jax.random.normal(ks[8], (D_MODEL,), dtype=jnp.float32) * s}
    _L0_attn_all = _L0_attn_setup()
    _L0_attn_in = {k: v for k, v in _L0_attn_all.items() if k in ('mask', 'Wq', 'bq', 'Wk', 'bk', 'Wv', 'bv', 'Wo', 'bo')}
    del _L0_attn_all

    def _L0_ffn_setup():
        import jax, jax.numpy as jnp
        import numpy as np
        E = 8
        TOP_K = 2
        D = 256
        H = 2 * D
        key = jax.random.key(seed)
        k0, k1, k2, k3, k4 = jax.random.split(key, 5)
        scale = 0.02
        x = jax.random.normal(k0, (4, 512, D), dtype=jnp.float32)
        Wg = jax.random.normal(k1, (D, E), dtype=jnp.float32) * scale
        W1 = jax.random.normal(k2, (E, D, H), dtype=jnp.float32) * scale
        W2 = jax.random.normal(k3, (E, D, H), dtype=jnp.float32) * scale
        W3 = jax.random.normal(k4, (E, H, D), dtype=jnp.float32) * scale
        return {'x': x, 'Wg': Wg, 'W1': W1, 'W2': W2, 'W3': W3}
    _L0_ffn_all = _L0_ffn_setup()
    _L0_ffn_in = {k: v for k, v in _L0_ffn_all.items() if k in ('Wg', 'W1', 'W2', 'W3')}
    del _L0_ffn_all
    return {'x': x, 'ctx_1024': ctx_1024, 'L0_xattn_wq': _L0_xattn_in['wq'], 'L0_xattn_wk': _L0_xattn_in['wk'], 'L0_xattn_wv': _L0_xattn_in['wv'], 'L0_xattn_wo': _L0_xattn_in['wo'], 'L0_xattn_bo': _L0_xattn_in['bo'], 'L0_attn_mask': _L0_attn_in['mask'], 'L0_attn_Wq': _L0_attn_in['Wq'], 'L0_attn_bq': _L0_attn_in['bq'], 'L0_attn_Wk': _L0_attn_in['Wk'], 'L0_attn_bk': _L0_attn_in['bk'], 'L0_attn_Wv': _L0_attn_in['Wv'], 'L0_attn_bv': _L0_attn_in['bv'], 'L0_attn_Wo': _L0_attn_in['Wo'], 'L0_attn_bo': _L0_attn_in['bo'], 'L0_ffn_Wg': _L0_ffn_in['Wg'], 'L0_ffn_W1': _L0_ffn_in['W1'], 'L0_ffn_W2': _L0_ffn_in['W2'], 'L0_ffn_W3': _L0_ffn_in['W3']}

def reference(x, ctx_1024, L0_xattn_wq, L0_xattn_wk, L0_xattn_wv, L0_xattn_wo, L0_xattn_bo, L0_attn_mask, L0_attn_Wq, L0_attn_bq, L0_attn_Wk, L0_attn_bk, L0_attn_Wv, L0_attn_bv, L0_attn_Wo, L0_attn_bo, L0_ffn_Wg, L0_ffn_W1, L0_ffn_W2, L0_ffn_W3):
    import jax
    import jax.numpy as jnp

    def _L0_xattn_ref(x1, x2, wq, wk, wv, wo, bo):
        import jax, jax.numpy as jnp
        import numpy as np
        DIM = 256
        HEADS = 16
        HEAD_DIM = DIM // HEADS
        SCALE = HEAD_DIM ** (-0.5)
        b, n, _ = x1.shape
        m = x2.shape[1]
        q = (x1 @ wq.T).reshape(b, n, HEADS, HEAD_DIM).transpose(0, 2, 1, 3)
        k = (x2 @ wk.T).reshape(b, m, HEADS, HEAD_DIM).transpose(0, 2, 1, 3)
        v = (x2 @ wv.T).reshape(b, m, HEADS, HEAD_DIM).transpose(0, 2, 1, 3)
        dots = jnp.einsum('bhnd,bhmd->bhnm', q, k) * SCALE
        attn = jax.nn.softmax(dots, axis=-1)
        out = jnp.einsum('bhnm,bhmd->bhnd', attn, v)
        out = out.transpose(0, 2, 1, 3).reshape(b, n, DIM)
        return out @ wo.T + bo

    def _L0_attn_ref(x, mask, Wq, bq, Wk, bk, Wv, bv, Wo, bo):
        import jax, jax.numpy as jnp
        import numpy as np
        D_MODEL = 256
        N_HEADS = 16
        D_HEAD = D_MODEL // N_HEADS
        EPS = 1e-06
        B, N = (1, 512)

        def _phi(x):
            return jax.nn.elu(x) + 1.0

        def _split_heads(y, b, n):
            return y.reshape(b, n, N_HEADS, D_HEAD).transpose(0, 2, 1, 3)
        b, n, _ = x.shape
        q = _phi(_split_heads(x @ Wq.T + bq, b, n))
        k = _phi(_split_heads(x @ Wk.T + bk, b, n))
        v = _split_heads(x @ Wv.T + bv, b, n)
        kv = jnp.einsum('bhnd,bhne->bhnde', k, v)
        kv_prefix = jnp.cumsum(kv, axis=2)
        k_prefix = jnp.cumsum(k, axis=2)
        numer = jnp.einsum('bhnd,bhnde->bhne', q, kv_prefix)
        denom = jnp.einsum('bhnd,bhnd->bhn', q, k_prefix)[..., None]
        out_heads = numer / (denom + EPS)
        merged = out_heads.transpose(0, 2, 1, 3).reshape(b, n, D_MODEL)
        return merged @ Wo.T + bo

    def _L0_ffn_ref(x, Wg, W1, W2, W3):
        import jax, jax.numpy as jnp
        import numpy as np
        E = 8
        TOP_K = 2
        D = 256
        H = 2 * D
        logits = jnp.einsum('bsd,de->bse', x, Wg)
        top_vals, top_idx = jax.lax.top_k(logits, TOP_K)
        probs = jax.nn.softmax(top_vals, axis=-1)
        onehot = jax.nn.one_hot(top_idx, E, dtype=x.dtype)
        weights = jnp.einsum('bsk,bske->bse', probs, onehot)
        out = jnp.zeros_like(x)
        for e in range(E):
            u = jnp.einsum('bsd,dh->bsh', x, W1[e])
            v = jnp.einsum('bsd,dh->bsh', x, W2[e])
            h = u * jax.nn.sigmoid(u) * v
            y = jnp.einsum('bsh,hd->bsd', h, W3[e])
            out = out + y * weights[..., e][..., None]
        return out
    x = x + _L0_xattn_ref(_layernorm(x, axis=-1), ctx_1024, L0_xattn_wq, L0_xattn_wk, L0_xattn_wv, L0_xattn_wo, L0_xattn_bo)
    x = x + _L0_attn_ref(_layernorm(x, axis=-1), L0_attn_mask, L0_attn_Wq, L0_attn_bq, L0_attn_Wk, L0_attn_bk, L0_attn_Wv, L0_attn_bv, L0_attn_Wo, L0_attn_bo)
    x = x + _L0_ffn_ref(_layernorm(x, axis=-1), L0_ffn_Wg, L0_ffn_W1, L0_ffn_W2, L0_ffn_W3)
    return x

_drawn_inputs = setup_inputs


def setup_inputs(seed=0):
    import zlib

    import numpy as np

    out = dict(_drawn_inputs(seed))
    spreads = {}
    factors = {'L0_xattn_bo': 5.092,
     'L0_attn_Wq': 2.767,
     'L0_attn_bq': 8.0,
     'L0_attn_bk': 8.0,
     'L0_ffn_Wg': 4.781,
     'L0_ffn_W1': 4.235,
     'L0_ffn_W2': 4.186,
     'L0_ffn_W3': 4.196}
    for name, (base, spread) in spreads.items():
        noise = np.random.default_rng([zlib.crc32(name.encode()), seed]).standard_normal(out[name].shape)
        drawn = base * np.exp(spread * noise) if base else spread * noise
        out[name] = jnp.asarray(drawn.astype(out[name].dtype))
    for name, factor in factors.items():
        out[name] = (out[name] * factor).astype(out[name].dtype)
    return out
```

```python
from contextlib import ExitStack

import concourse.bass as bass
from concourse import mybir

B, NQ, D = 128, 32, 256
M = 257
H, HD = 16, 16
E, F = 8, 512
P = 128
TOK = B * NQ
TILES = TOK // P
BT = P // NQ
C = D // P
G = 4
JH = H // G
UNITS = BT * G
FC = F // P
REGION = TOK + P
TOPK = 2
MOE_TILES = TOPK * TOK // P + E - 1
LN_EPS = 1e-5
ATT_EPS = 1e-6
WQ1, WK1, WV1, WO1, WQ2, WK2, WV2, WO2 = range(8)
P_SLOTS = 8


def first(t):
    return isinstance(t, int) and t == 0


def perceiver(nc, x, ctx_t, tail_t, w_attn, bias_rows, bias_qk, wg, w1, w2, w3,
              ident, head_mask, fold_mask, causal, tri, expand, query_eye, expert_row, tile_row,
              routed, hidden, x2_dram, out):
    f32 = mybir.dt.float32
    i32 = mybir.dt.int32
    u32 = mybir.dt.uint32
    ACT = mybir.ActivationFunctionType
    ALU = mybir.AluOpType
    AX = mybir.AxisListType.X

    with ExitStack() as stack:
        def sb(name, shape, dt=f32):
            return stack.enter_context(nc.sbuf_tensor(name, shape, dt))

        def sem(name):
            return stack.enter_context(nc.semaphore(name))

        ident_sb = sb("ident_sb", [P, P])
        head_mask_sb = sb("head_mask_sb", [P, 2 * JH])
        scaled_mask_sb = sb("scaled_mask_sb", [P, 2 * JH])
        fold_mask_sb = sb("fold_mask_sb", [P, JH])
        causal_sb = sb("causal_sb", [P, P])
        tri_sb = sb("tri_sb", [P, 2, P])
        expand_sb = sb("expand_sb", [P, 2, P])
        query_eye_sb = sb("query_eye_sb", [P, NQ])
        expert_row_sb = sb("expert_row_sb", [P, 2, E])
        tile_row_sb = sb("tile_row_sb", [P, MOE_TILES])
        w_sb = sb("w_sb", [P, 8, C, D])
        bias_sb = sb("bias_sb", [P, 3, D])
        bias_qk_sb = sb("bias_qk_sb", [P, 4])
        wg_sb = sb("wg_sb", [P, C, E])
        w1_sb = sb("w1_sb", [P, E, C, F])
        w2_sb = sb("w2_sb", [P, E, C, F])
        w3_sb = sb("w3_sb", [P, E, FC, D])
        neg_half = sb("neg_half", [P, 1])
        tail_sb = sb("tail_sb", [P, C, B])
        v_tail = sb("v_tail", [P, C, B])

        ctx_sb = sb("ctx_sb", [P, BT, C, M])
        k_t = sb("k_t", [P, 2, C, M])
        v_sb = sb("v_sb", [P, 2, 2, D])
        x_ln1 = sb("x_ln1", [P, D])
        xn1 = sb("xn1", [P, D])
        xn1_t = sb("xn1_t", [P, C, P])
        q_t = sb("q_t", [P, C, P])
        q_heads = sb("q_heads", [P, 2, C, 2 * JH, NQ])
        neg_max = sb("neg_max", [P, UNITS])
        prob = sb("prob", [P, P_SLOTS, M])
        row_stat = sb("row_stat", [P, G, 2, BT])
        prob_t = sb("prob_t", [P, 2, 2, P])
        o_masked = sb("o_masked", [P, C, JH, NQ])
        o_t = sb("o_t", [P, C, BT, NQ])
        stat_rows = sb("stat_rows", [P, G, 2 * BT, NQ])
        recip_sum = sb("recip_sum", [P, C, P])
        o_tail = sb("o_tail", [P, C, P])
        o_norm = sb("o_norm", [P, C, P])

        x_res = sb("x_res", [P, D])
        x1 = sb("x1", [P, D])
        xn2 = sb("xn2", [P, D])
        xn2_t = sb("xn2_t", [P, C, P])
        qk_pre = sb("qk_pre", [P, 4, P])
        qk_min = sb("qk_min", [P, 4, P])
        qk_phi = sb("qk_phi", [P, 4, P])
        v_aug = sb("v_aug", [P, H, HD + 1])
        phi_heads = sb("phi_heads", [P, C, 2 * JH, P])
        a_t = sb("a_t", [P, H, P])
        den = sb("den", [P, H])
        merged = sb("merged", [P, H, HD])
        merged_t = sb("merged_t", [P, C, P])
        x2 = sb("x2", [P, D])
        xn3 = sb("xn3", [P, D])
        xn3_t = sb("xn3_t", [P, C, P])
        ln = [sb(f"ln{k}", [P, 16]) for k in range(3)]

        logits = sb("logits", [P, E])
        top = sb("top", [P, E])
        top_at = sb("top_at", [P, E], u32)
        top_f = sb("top_f", [P, TOPK])
        chosen = sb("chosen", [P, TOPK, E])
        chosen_any = sb("chosen_any", [P, E])
        row_next = sb("row_next", [P, E])
        pos = sb("pos", [P, E])
        pos_chosen = sb("pos_chosen", [P, TOPK, E])
        slot_f = sb("slot_f", [P, TOPK])
        slot = sb("slot", [P, TOPK], i32)
        slots = sb("slots", [P, TILES, TOPK])
        experts = sb("experts", [P, TILES, TOPK])
        behind = sb("behind", [P, TILES, TOPK])
        packed = sb("packed", [P, TILES, TOPK], i32)
        pick_at = sb("pick_at", [P, 2, TOPK], i32)
        tops = sb("tops", [P, TILES, TOPK])
        plan = sb("plan", [P, 8, MOE_TILES])
        plan_i = sb("plan_i", [P, 3, MOE_TILES], i32)
        weight = sb("weight", [P, TOPK, TILES])

        zeros = sb("zeros", [P, D])
        xe = sb("xe", [P, D])
        xe_t = sb("xe_t", [P, C, P])
        spare_a = phi_heads[:].rearrange("p c j n -> p (c j n)")
        spare_b = a_t[:].rearrange("p h n -> p (h n)")
        gate, hid = spare_a[:, 0:F], spare_a[:, F:2 * F]
        hid_t = spare_a[:, 2 * F:3 * F].rearrange("p (c n) -> p c n", c=FC)
        ye = spare_a[:, 3 * F:3 * F + D]
        y_pick = spare_b[:, 0:4 * D].rearrange("p (s r d) -> p s r d", s=2, r=TOPK)
        x2_back = spare_b[:, 4 * D:6 * D].rearrange("p (s d) -> p s d", s=2)
        y_out = spare_b[:, 6 * D:8 * D].rearrange("p (s d) -> p s d", s=2)

        bank = [stack.enter_context(nc.psum_tensor(f"bank{k}", [P, 512], f32)) for k in range(8)]
        proj_ps = bank[0:2]
        score_ps = bank[2:4]
        pt_ps, o_ps, c_ps, f_ps = bank[4:8]

        consts_in = sem("consts_in")
        experts_in = sem("experts_in")
        tail_done, tail_out = sem("tail_done"), sem("tail_out")
        ctx_in = [sem(f"ctx_in{b}") for b in range(BT)]
        xln_in, xres_in = sem("xln_in"), sem("xres_in")
        proj_done, proj_out = sem("proj_done"), sem("proj_out")
        score_done, max_done, exp_done = sem("score_done"), sem("max_done"), sem("exp_done")
        pt_done, pt_out, pv_done, o_out = sem("pt_done"), sem("pt_out"), sem("pv_done"), sem("o_out")
        o_step = sem("o_step")
        heads_done = sem("heads_done")
        last_copied, stats_done = sem("last_copied"), sem("stats_done")
        ln_step = [sem(f"ln_step{k}") for k in range(3)]
        ln_var = [sem(f"ln_var{k}") for k in range(3)]
        ln_eps_done = [sem(f"ln_eps_done{k}") for k in range(3)]
        ln_rstd = [sem(f"ln_rstd{k}") for k in range(3)]
        ln_out = [sem(f"ln_out{k}") for k in range(3)]
        xt_done = [sem(f"xt_done{k}") for k in range(3)]
        xt_out = [sem(f"xt_out{k}") for k in range(3)]
        q_done, q_out = sem("q_done"), sem("q_out")
        ex_done, ex_step, norm_out = sem("ex_done"), sem("ex_step"), sem("norm_out")
        wo1_done, xb_done, x1_out, x1b_done = sem("wo1_done"), sem("xb_done"), sem("x1_out"), sem("x1b_done")
        qk_done, v2_done, v2_out = sem("qk_done"), sem("v2_done"), sem("v2_out")
        qkb_step, qkb_out, qke_out, phi_out, phiq_out = (sem("qkb_step"), sem("qkb_out"), sem("qke_out"),
                                                         sem("phi_out"), sem("phiq_out"))
        sc2_done, sc2_out = sem("sc2_done"), sem("sc2_out")
        av_done, av_step, merged_out = sem("av_done"), sem("av_step"), sem("merged_out")
        mt_done, mt_out = sem("mt_done"), sem("mt_out")
        wo2_done, x2_out, x2_stored = sem("wo2_done"), sem("x2_out"), sem("x2_stored")
        lg_done, lg_step, any_out, rank_done, rank_step, slot_out = (
            sem("lg_done"), sem("lg_step"), sem("any_out"), sem("rank_done"), sem("rank_step"), sem("slot_out"))
        routed_out = sem("routed_out")
        setup = sem("setup")
        packed_out = sem("packed_out")
        plan_step, plan_out, zero_in = sem("plan_step"), sem("plan_out"), sem("zero_in")
        weight_exp, weight_out = sem("weight_exp"), sem("weight_out")
        xe_in, xet_done, xet_out = sem("xe_in"), sem("xet_done"), sem("xet_out")
        u_done, gv_done, sig_out, hid_step, hid_out = (sem("u_done"), sem("gv_done"), sem("sig_out"),
                                                       sem("hid_step"), sem("hid_out"))
        ht_done, ht_out, y_done, ye_out, ye_stored = (sem("ht_done"), sem("ht_out"), sem("y_done"),
                                                      sem("ye_out"), sem("ye_stored"))
        pick_ready = sem("pick_ready")
        waits_passed = sem("waits_passed")
        picked = [sem(f"picked{s}") for s in range(2)]
        back_in = [sem(f"back_in{s}") for s in range(2)]
        sum_step, sum_out = sem("sum_step"), sem("sum_out")
        stored = [sem(f"stored{s}") for s in range(2)]
        CONSTS = 16 * 17
        EXPERTS = 16 * 3

        block = stack.enter_context(nc.Block())

        def phases(i):
            if not isinstance(i, int):
                return True, True, True, True
            return i < TILES, i + 1 < TILES, 1 <= i <= TILES, 2 <= i <= TILES + 1

        def apart(engine):
            engine.sem_inc(waits_passed, 1)

        def iterations(engine, body):
            for i in range(3):
                body(i)
            with engine.Fori(3, TILES - 1) as i:
                body(i)
            for i in range(TILES - 1, TILES + 2):
                body(i)

        @block.sync
        def _(sp):
            def load_ctx(t, b):
                if not first(t):
                    sp.wait_ge(proj_done, ((t - 1) * BT + b + 1) * 3)
                sp.dma_start(ctx_sb[:, b], ctx_t[t, b]).then_inc(ctx_in[b], 16)

            def load_xln(t):
                if not first(t):
                    sp.wait_ge(ln_out[0], t)
                sp.dma_start(x_ln1[:], x[t]).then_inc(xln_in, 16)

            def load_xres(t):
                if not first(t):
                    sp.wait_ge(x1_out, t)
                sp.dma_start(x_res[:], x[t]).then_inc(xres_in, 16)

            sp.dma_start(w_sb[:], w_attn).then_inc(consts_in, 16)
            load_xln(0)
            for b in range(BT):
                load_ctx(0, b)
            sp.dma_start(tail_sb[:], tail_t).then_inc(consts_in, 16)
            for k in range(3):
                sp.dma_start(bias_sb[:, k], bias_rows[k:k + 1, :].broadcast_to([P, D])).then_inc(consts_in, 16)
            load_xres(0)

            def body(i):
                att, nxt, rest, route = phases(i)
                if nxt:
                    load_xln(i + 1)
                if nxt:
                    for b in range(BT):
                        load_ctx(i + 1, b)
                if rest and nxt:
                    load_xres(i)
                if isinstance(i, int) and i == TILES - 1:
                    load_xres(i)
                if rest:
                    sp.wait_ge(x2_out, i)
                    sp.dma_start(x2_dram[i - 1], x2[:]).then_inc(x2_stored, 16)
                if isinstance(i, int) and i == 1:
                    sp.dma_start(w1_sb[:], w1).then_inc(experts_in, 16)
                    sp.dma_start(w2_sb[:], w2).then_inc(experts_in, 16)
                    sp.dma_start(w3_sb[:], w3).then_inc(experts_in, 16)
            iterations(sp, body)

            sp.wait_ge(plan_out, 1)
            sp.wait_ge(routed_out, 32 * TILES)
            for e in range(E):
                row = sp.value_load(plan_i[0:1, 2, e:e + 1], min_val=0, max_val=E * REGION - P)
                sp.dma_start(routed[bass.ds(row, P), :], zeros[:]).then_inc(zero_in, 16)
            sp.wait_ge(zero_in, 16 * E)

            def load_tile(t):
                if not first(t):
                    sp.wait_ge(xet_done, t)
                row = sp.value_load(plan_i[0:1, 1, bass.ds(t, 1)], min_val=0, max_val=E * REGION - P)
                sp.dma_start(xe[:], routed[bass.ds(row, P), :]).then_inc(xe_in, 16)

            def store_tile(t):
                sp.wait_ge(ye_out, t + 1)
                sp.dma_start(hidden[t * P:(t + 1) * P, :] if isinstance(t, int) else hidden[bass.ds(t * P, P), :],
                             ye).then_inc(ye_stored, 16)

            load_tile(0)
            load_tile(1)
            with sp.Fori(2, MOE_TILES) as t:
                load_tile(t)
                store_tile(t - 2)
            store_tile(MOE_TILES - 2)
            store_tile(MOE_TILES - 1)

            def load_back(t, s):
                if not (isinstance(t, int) and t < 2):
                    sp.wait_ge(sum_out, t - 1)
                sp.dma_start(x2_back[:, s], x2_dram[t]).then_inc(back_in[s], 16)

            sp.wait_ge(x2_stored, 16 * TILES)
            for s in range(2):
                load_back(s, s)
            with sp.Fori(1, TILES // 2) as r:
                for s in range(2):
                    load_back(2 * r + s, s)

        @block.scalar
        def _(act):
            for dst, src in ((ident_sb[:], ident), (head_mask_sb[:], head_mask),
                             (fold_mask_sb[:], fold_mask), (causal_sb[:], causal), (tri_sb[:], tri),
                             (expand_sb[:], expand), (query_eye_sb[:], query_eye),
                             (expert_row_sb[:], expert_row), (tile_row_sb[:], tile_row),
                             (bias_qk_sb[:], bias_qk), (wg_sb[:], wg)):
                act.dma_start(dst, src).then_inc(consts_in, 16)
            act.dma_start(scaled_mask_sb[:], head_mask).then_inc(consts_in, 16)
            act.wait_ge(tail_done, 1)
            nc.scalar.copy(v_tail[:], f_ps[:, 0:C * B].rearrange("p (c b) -> p c b", c=C)).then_inc(tail_out, 1)

            def copy_proj(t, b, k):
                n = (t * BT + b) * 3 + k
                bank_of = proj_ps[(b * 3 + k) % 2]
                act.wait_ge(proj_done, n + 1)
                if k < 2:
                    nc.scalar.copy(k_t[:, b % 2, k], bank_of[:, 0:M]).then_inc(proj_out, 1)
                else:
                    nc.scalar.copy(v_sb[:, b % 2], bank_of[:].rearrange("p (m d) -> p m d", m=2))\
                        .then_inc(proj_out, 1)

            def copy_xt(t, k, dst, src):
                act.wait_ge(xt_done[k], t + 1)
                nc.scalar.copy(dst[:], src[:, 0:C * P].rearrange("p (c n) -> p c n", c=C)).then_inc(xt_out[k], 1)

            def copy_q(t):
                act.wait_ge(q_done, t + 1)
                if not first(t):
                    act.wait_ge(heads_done, t * BT)
                nc.scalar.copy(q_t[:], f_ps[:, 0:C * P].rearrange("p (c n) -> p c n", c=C)).then_inc(q_out, 1)

            def exponentials(t, u):
                b, g = u // G, u % G
                n = t * UNITS + u
                act.wait_ge(max_done, n + 1)
                if not (isinstance(t, int) and n < P_SLOTS):
                    act.wait_ge(pt_done, n - P_SLOTS + 1)
                    if g == 0:
                        act.wait_ge(last_copied, t * BT + b - 1)
                if u == 0 and not first(t):
                    act.wait_ge(stats_done, t)
                nc.scalar.activation(prob[:, u % P_SLOTS], score_ps[u % 2][:, 0:M], ACT.Exp,
                                     bias=neg_max[:, u:u + 1], scale=1.0,
                                     accum_out=row_stat[:, g, 0, b:b + 1]).then_inc(exp_done, 1)

            copy_xt(0, 0, xn1_t, f_ps)
            copy_q(0)
            for k in range(3):
                copy_proj(0, 0, k)

            def body(i):
                att, nxt, rest, route = phases(i)
                for u in range(UNITS):
                    b, g = u // G, u % G
                    if att:
                        exponentials(i, u)
                        if g < 3 and b < 3:
                            copy_proj(i, b + 1, g)
                        elif g < 3 and nxt:
                            copy_proj(i + 1, 0, g)
                    if rest and u == 6:
                        copy_xt(i - 1, 1, xn2_t, c_ps)
                    if nxt and u == 5:
                        copy_xt(i + 1, 0, xn1_t, f_ps)
                    if rest and u == 8:
                        act.wait_ge(qkb_out, i)
                        nc.scalar.activation(qk_min[:], qk_min[:], ACT.Exp).then_inc(qke_out, 1)
                    if rest and u == 13:
                        act.wait_ge(mt_done, i)
                        nc.scalar.copy(merged_t[:], c_ps[:, 0:C * P].rearrange("p (c n) -> p c n", c=C))\
                            .then_inc(mt_out, 1)
                    if nxt and u == 14:
                        copy_q(i + 1)
                    if rest and u == 15:
                        copy_xt(i - 1, 2, xn3_t, c_ps)
            iterations(act, body)

            act.wait_ge(weight_exp, 1)
            nc.scalar.activation(weight[:, 1], weight[:, 1], ACT.Exp).then_inc(weight_exp, 1)

            def expert_tile(t):
                act.wait_ge(u_done, t + 1)
                if not first(t):
                    act.wait_ge(hid_out, t)
                nc.scalar.activation(gate, bank[0][:], ACT.Sigmoid).then_inc(sig_out, 1)

            def copy_hid(t):
                act.wait_ge(ht_done, t + 1)
                nc.scalar.copy(hid_t, bank[3][:].rearrange("p (c n) -> p c n", c=FC)).then_inc(ht_out, 1)

            expert_tile(0)
            with act.Fori(1, MOE_TILES) as t:
                expert_tile(t)
                copy_hid(t - 1)
            copy_hid(MOE_TILES - 1)

            def store(t, s):
                act.wait_ge(sum_out, t + 1)
                act.dma_start(out[t], y_out[:, s]).then_inc(stored[s], 16)

            with act.Fori(0, TILES // 2) as r:
                for s in range(2):
                    store(2 * r + s, s)
            for s in range(2):
                act.wait_ge(stored[s], 16 * (TILES // 2))

        @block.gpsimd
        def _(pool):
            nc.gpsimd.memset(neg_half[:], -0.5).then_inc(setup, 1)
            nc.gpsimd.memset(zeros[:], 0.0).then_inc(setup, 1)
            nc.gpsimd.memset(v_aug[:], 1.0).then_inc(setup, 1)
            pool.wait_ge(setup, 3)
            pool.wait_ge(consts_in, CONSTS)
            nc.gpsimd.tensor_scalar(scaled_mask_sb[:], head_mask_sb[:], float(HD) ** -0.5, None, ALU.mult)\
                .then_inc(setup, 1)
            pool.wait_ge(setup, 4)

            def rstd(t, k):
                pool.wait_ge(ln_var[k], t + 1)
                apart(pool)
                nc.gpsimd.tensor_scalar(ln[k][:, 9:10], ln[k][:, 7:8], LN_EPS, None, ALU.add)\
                    .then_inc(ln_eps_done[k], 1)
                pool.wait_ge(ln_eps_done[k], t + 1)
                nc.gpsimd.tensor_tensor(ln[k][:, 8:9], ln[k][:, 9:10], neg_half[:], ALU.pow)\
                    .then_inc(ln_rstd[k], 1)

            def split_heads(t, b):
                n = t * BT + b
                pool.wait_ge(q_out, t + 1)
                if not (isinstance(t, int) and n < 2):
                    pool.wait_ge(score_done, (n - 1) * G)
                src = q_t[:, :, b * NQ:(b + 1) * NQ].unsqueeze(2).broadcast_to([P, C, 2 * JH, NQ])
                msk = scaled_mask_sb[:].unsqueeze(1).unsqueeze(3).broadcast_to([P, C, 2 * JH, NQ])
                nc.gpsimd.tensor_tensor(q_heads[:, b % 2], src, msk, ALU.mult).then_inc(heads_done, 1)

            def last_column(t, b):
                pool.wait_ge(exp_done, (t * BT + b + 1) * G)
                if b == 0 and not first(t):
                    pool.wait_ge(stats_done, t)
                s = (b * G) % P_SLOTS
                apart(pool)
                nc.gpsimd.tensor_copy(row_stat[:, :, 1, b], prob[:, s:s + G, M - 1]).then_inc(last_copied, 1)

            rstd(0, 0)
            split_heads(0, 0)

            def body(i):
                att, nxt, rest, route = phases(i)
                for u in range(UNITS):
                    b, g = u // G, u % G
                    if att and g == 1 and b < 3:
                        split_heads(i, b + 1)
                    if nxt and u == 15:
                        split_heads(i + 1, 0)
                    if att and g == 3 and b < 3:
                        last_column(i, b)
                    if rest and u == 0:
                        last_column(i - 1, 3)
                        pool.wait_ge(last_copied, i * BT)
                        if not (isinstance(i, int) and i < 2):
                            pool.wait_ge(ex_done, i - 1)
                        src = row_stat[:].rearrange("p g w b -> p (g w b)").unsqueeze(2)\
                            .broadcast_to([P, G * 2 * BT, NQ])
                        eye = query_eye_sb[:].unsqueeze(1).broadcast_to([P, G * 2 * BT, NQ])
                        nc.gpsimd.tensor_tensor(stat_rows[:].rearrange("p g w n -> p (g w) n"), src, eye,
                                                ALU.mult).then_inc(stats_done, 1)
                    if rest and u == 1:
                        pool.wait_ge(xres_in, i * 16)
                        nc.gpsimd.tensor_tensor(x_res[:], x_res[:], bias_sb[:, 0], ALU.add).then_inc(xb_done, 1)
                    if nxt and u == 2:
                        rstd(i + 1, 0)
                    if rest and u == 4:
                        rstd(i - 1, 1)
                    if rest and u == 8:
                        pool.wait_ge(phi_out, i)
                        if not (isinstance(i, int) and i < 2):
                            pool.wait_ge(sc2_done, (i - 1) * G)
                        src = qk_phi[:, 0:C].unsqueeze(2).broadcast_to([P, C, 2 * JH, P])
                        msk = head_mask_sb[:].unsqueeze(1).unsqueeze(3).broadcast_to([P, C, 2 * JH, P])
                        nc.gpsimd.tensor_tensor(phi_heads[:], src, msk, ALU.mult).then_inc(phiq_out, 1)
                    if rest and u == 10:
                        pool.wait_ge(x1_out, i)
                        pool.wait_ge(ln_out[1], i)
                        nc.gpsimd.tensor_tensor(x1[:], x1[:], bias_sb[:, 2], ALU.add).then_inc(x1b_done, 1)
                    if rest and u == 14:
                        rstd(i - 1, 2)
                    if route and u == 4:
                        pool.wait_ge(slot_out, i - 1)
                        for r in range(TOPK):
                            apart(pool)
                            pool.indirect_dma_start(
                                routed, bass.IndirectOffsetOnAxis(ap=slot[:, r:r + 1], axis=0), xn3[:], None)\
                                .then_inc(routed_out, 16)
                        pool.wait_ge(routed_out, 32 * (i - 1))
            iterations(pool, body)

            def pick(t, s):
                if not (isinstance(t, int) and t < 2):
                    pool.wait_ge(sum_out, t - 1)
                apart(pool)
                nc.gpsimd.tensor_copy(pick_at[:, s], packed[:, bass.ds(t, 1)].rearrange("p a k -> p (a k)"))\
                    .then_inc(pick_ready, 1)
                pool.wait_ge(pick_ready, t + 1)
                for r in range(TOPK):
                    apart(pool)
                    pool.indirect_dma_start(
                        y_pick[:, s, r], None, hidden,
                        bass.IndirectOffsetOnAxis(ap=pick_at[:, s, r:r + 1], axis=0)).then_inc(picked[s], 16)

            pool.wait_ge(packed_out, 1)
            pool.wait_ge(ye_stored, 16 * MOE_TILES)
            for s in range(2):
                pick(s, s)
            with pool.Fori(1, TILES // 2) as r:
                for s in range(2):
                    pick(2 * r + s, s)

        @block.vector
        def _(dve):
            dve.wait_ge(setup, 4)
            dve.wait_ge(consts_in, CONSTS)
            nc.vector.tensor_copy(row_next[:], expert_row_sb[:, 1]).then_inc(setup, 1)

            def norm_stats(t, k, src):
                nc.vector.bn_stats(ln[k][:, 0:6], src).then_inc(ln_step[k], 1)
                dve.wait_ge(ln_step[k], t + 1)
                apart(dve)
                nc.vector.bn_aggr(ln[k][:, 6:8], ln[k][:, 0:6]).then_inc(ln_var[k], 1)

            def norm_scale(t, k, src, dst):
                dve.wait_ge(ln_rstd[k], t + 1)
                nc.vector.tensor_scalar(dst, src, ln[k][:, 6:7], ln[k][:, 8:9], ALU.subtract, ALU.mult)\
                    .then_inc(ln_out[k], 1)

            def negative_max(t, u):
                dve.wait_ge(score_done, t * UNITS + u + 1)
                nc.vector.tensor_reduce(neg_max[:, u:u + 1], score_ps[u % 2][:, 0:M], AX, ALU.max, negate=True)\
                    .then_inc(max_done, 1)

            def copy_pt(t, u):
                n = t * UNITS + u
                dve.wait_ge(pt_done, n + 1)
                if not (isinstance(t, int) and n < 2):
                    dve.wait_ge(pv_done, n - 1)
                nc.vector.tensor_copy(prob_t[:, u % 2], pt_ps[:, 0:2 * P].rearrange("p (m n) -> p m n", m=2))\
                    .then_inc(pt_out, 1)

            def fold_o(t, b):
                n = t * BT + b
                dve.wait_ge(pv_done, (n + 1) * G)
                ps = o_ps[:, 0:C * P].rearrange("p (c j n) -> p c j n", c=C, j=JH)
                msk = fold_mask_sb[:].unsqueeze(1).unsqueeze(3).broadcast_to([P, C, JH, NQ])
                nc.vector.tensor_tensor(o_masked[:], ps, msk, ALU.mult).then_inc(o_out, 1)
                dve.wait_ge(o_out, n + 1)
                nc.vector.tensor_reduce(o_t[:, :, b], o_masked[:].rearrange("p c j n -> p c n j"), AX, ALU.add)\
                    .then_inc(o_step, 1)

            norm_src = x_ln1[:]
            dve.wait_ge(xln_in, 16)
            norm_stats(0, 0, norm_src)
            norm_scale(0, 0, norm_src, xn1[:])

            def body(i):
                att, nxt, rest, route = phases(i)
                for u in range(UNITS):
                    if att:
                        negative_max(i, u)
                    if att and u >= 1:
                        copy_pt(i, u - 1)
                    if rest and u == 0:
                        copy_pt(i - 1, UNITS - 1)
                    if att and u >= 2 and (u - 2) % G == 3:
                        fold_o(i, (u - 2) // G)
                    if rest and u == 1:
                        fold_o(i - 1, BT - 1)
                    if nxt and u == 2:
                        dve.wait_ge(xln_in, 16 * (i + 2))
                        norm_stats(i + 1, 0, x_ln1[:])
                    if nxt and u == 3:
                        dve.wait_ge(xt_done[0], i + 1)
                        norm_scale(i + 1, 0, x_ln1[:], xn1[:])
                    if rest and u == 2:
                        t = i - 1
                        dve.wait_ge(ex_done, t + 1)
                        dve.wait_ge(o_step, (t + 1) * BT)
                        ex = c_ps[:].rearrange("p (c w n) -> p c w n", c=C, w=2)
                        ext = c_ps[:].rearrange("p (c w b n) -> p c w b n", c=C, w=2, b=BT)
                        nc.vector.reciprocal(recip_sum[:], ex[:, :, 0]).then_inc(ex_step, 1)
                        vt = v_tail[:, :, bass.ds(t * BT, BT)].unsqueeze(3).broadcast_to([P, C, BT, NQ])
                        nc.vector.tensor_tensor(o_tail[:].rearrange("p c (b n) -> p c b n", b=BT),
                                                ext[:, :, 1], vt, ALU.mult).then_inc(ex_step, 1)
                        dve.wait_ge(ex_step, t * 3 + 2)
                        nc.vector.tensor_tensor(o_tail[:], o_tail[:], o_t[:].rearrange("p c b n -> p c (b n)"),
                                                ALU.add).then_inc(ex_step, 1)
                        dve.wait_ge(ex_step, t * 3 + 3)
                        nc.vector.tensor_tensor(o_norm[:], o_tail[:], recip_sum[:], ALU.mult)\
                            .then_inc(norm_out, 1)
                    if rest and u == 3:
                        dve.wait_ge(wo1_done, i)
                        dve.wait_ge(xb_done, i)
                        nc.vector.tensor_tensor(x1[:], c_ps[:, 0:D], x_res[:], ALU.add).then_inc(x1_out, 1)
                        dve.wait_ge(x1_out, i)
                        norm_stats(i - 1, 1, x1[:])
                    if rest and u == 4:
                        norm_scale(i - 1, 1, x1[:], xn2[:])
                    if rest and u == 7:
                        t = i - 1
                        dve.wait_ge(qk_done, t + 1)
                        bqk = bias_qk_sb[:].unsqueeze(2).broadcast_to([P, 4, P])
                        nc.vector.tensor_tensor(qk_pre[:], c_ps[:].rearrange("p (k n) -> p k n", k=4), bqk, ALU.add)\
                            .then_inc(qkb_step, 1)
                        dve.wait_ge(qkb_step, t + 1)
                        nc.vector.tensor_scalar(qk_min[:], qk_pre[:], 0.0, None, ALU.min).then_inc(qkb_out, 1)
                        dve.wait_ge(v2_done, t + 1)
                        if not first(t):
                            dve.wait_ge(av_done, t)
                        nc.vector.tensor_tensor(v_aug[:, :, 0:HD], f_ps[:, 0:D].rearrange("p (h d) -> p h d", h=H),
                                                bias_sb[:, 1].rearrange("p (h d) -> p h d", h=H), ALU.add)\
                            .then_inc(v2_out, 1)
                    if rest and u == 8:
                        dve.wait_ge(qke_out, i)
                        nc.vector.scalar_tensor_tensor(qk_phi[:], qk_pre[:], 0.0, qk_min[:], ALU.max, ALU.add)\
                            .then_inc(phi_out, 1)
                    if rest and u in (10, 11):
                        t = i - 1
                        for g in (2 * (u - 10), 2 * (u - 10) + 1):
                            dve.wait_ge(sc2_done, t * G + g + 1)
                            src = (c_ps, f_ps)[g % 2][:].rearrange("p (j n) -> p j n", j=JH)
                            nc.vector.tensor_tensor(a_t[:, g * JH:(g + 1) * JH], src,
                                                    causal_sb[:].unsqueeze(1).broadcast_to([P, JH, P]), ALU.mult)\
                                .then_inc(sc2_out, 1)
                    if rest and u == 12:
                        t = i - 1
                        dve.wait_ge(av_done, t + 1)
                        ps = c_ps[:, 0:H * (HD + 1)].rearrange("p (h d) -> p h d", h=H)
                        nc.vector.tensor_scalar(den[:], ps[:, :, HD], ATT_EPS, None, ALU.add).then_inc(av_step, 1)
                        dve.wait_ge(av_step, t * 2 + 1)
                        nc.vector.reciprocal(den[:], den[:]).then_inc(av_step, 1)
                        dve.wait_ge(av_step, t * 2 + 2)
                        nc.vector.tensor_tensor(merged[:], ps[:, :, 0:HD],
                                                den[:].unsqueeze(2).broadcast_to([P, H, HD]), ALU.mult)\
                            .then_inc(merged_out, 1)
                    if rest and u == 14:
                        t = i - 1
                        dve.wait_ge(wo2_done, t + 1)
                        dve.wait_ge(x1b_done, t + 1)
                        if not first(t):
                            dve.wait_ge(x2_stored, 16 * t)
                            dve.wait_ge(routed_out, 32 * t)
                        nc.vector.tensor_tensor(x2[:], c_ps[:, 0:D], x1[:], ALU.add).then_inc(x2_out, 1)
                        dve.wait_ge(x2_out, t + 1)
                        norm_stats(t, 2, x2[:])
                        norm_scale(t, 2, x2[:], xn3[:])
                    if route and u == 0:
                        r = i - 2
                        dve.wait_ge(lg_done, r + 1)
                        nc.vector.tensor_copy(logits[:], f_ps[:, 0:E]).then_inc(lg_step, 1)
                        dve.wait_ge(lg_step, r * 5 + 1)
                        apart(dve)
                        nc.vector.max(top[:], logits[:]).then_inc(lg_step, 1)
                        dve.wait_ge(lg_step, r * 5 + 2)
                        apart(dve)
                        nc.vector.max_index(top_at[:], top[:], logits[:]).then_inc(lg_step, 1)
                        nc.vector.tensor_copy(tops[:, bass.ds(r, 1)].rearrange("p a k -> p (a k)"), top[:, 0:TOPK])
                        dve.wait_ge(lg_step, r * 5 + 3)
                        nc.vector.tensor_copy(top_f[:], top_at[:, 0:TOPK]).then_inc(lg_step, 1)
                        dve.wait_ge(lg_step, r * 5 + 4)
                        nc.vector.tensor_copy(experts[:, bass.ds(r, 1)].rearrange("p a k -> p (a k)"), top_f[:])
                        nc.vector.tensor_tensor(chosen[:],
                                                expert_row_sb[:, 0].unsqueeze(1).broadcast_to([P, TOPK, E]),
                                                top_f[:].unsqueeze(2).broadcast_to([P, TOPK, E]), ALU.is_equal)\
                            .then_inc(lg_step, 1)
                        dve.wait_ge(lg_step, r * 5 + 5)
                        nc.vector.tensor_tensor(chosen_any[:], chosen[:, 0], chosen[:, 1], ALU.add)\
                            .then_inc(any_out, 1)
                    if route and u == 2:
                        r = i - 2
                        dve.wait_ge(rank_done, r + 1)
                        nc.vector.tensor_tensor(pos[:], f_ps[:, 0:E], row_next[:], ALU.add).then_inc(rank_step, 1)
                        dve.wait_ge(rank_step, r * 4 + 1)
                        nc.vector.tensor_tensor(row_next[:], f_ps[:, E:2 * E], row_next[:], ALU.add)\
                            .then_inc(rank_step, 1)
                        nc.vector.tensor_tensor(pos_chosen[:], chosen[:],
                                                pos[:].unsqueeze(1).broadcast_to([P, TOPK, E]), ALU.mult)\
                            .then_inc(rank_step, 1)
                        dve.wait_ge(rank_step, r * 4 + 3)
                        nc.vector.tensor_reduce(slot_f[:], pos_chosen[:], AX, ALU.add).then_inc(rank_step, 1)
                        dve.wait_ge(rank_step, r * 4 + 4)
                        nc.vector.tensor_copy(slots[:, bass.ds(r, 1)].rearrange("p a k -> p (a k)"), slot_f[:])
                        nc.vector.tensor_copy(slot[:], slot_f[:]).then_inc(slot_out, 1)
            iterations(dve, body)

            n_steps = [0]

            def step(ins):
                n_steps[0] += 1
                ins.then_inc(plan_step, 1)
                dve.wait_ge(plan_step, n_steps[0])

            count, n_tiles, end, skip = (plan[:, k, 0:E] for k in range(4))
            expert_of, row_of, passed, jump = (plan[:, k] for k in range(4, 8))
            base = expert_row_sb[:, 1]
            taken = plan_i[:, 2, 0:E]
            dve.wait_ge(rank_step, 4 * TILES)
            step(nc.vector.tensor_copy(taken, row_next[:]))
            step(nc.vector.tensor_tensor(count, row_next[:], base, ALU.subtract))
            step(nc.vector.tensor_scalar(count, count, float(P - 1), None, ALU.add))
            tiles_i = plan_i[:, 0, 0:E]
            step(nc.vector.tensor_copy(tiles_i, count))
            step(nc.vector.tensor_scalar(tiles_i, tiles_i, 7, None, ALU.logical_shift_right))
            step(nc.vector.tensor_copy(n_tiles, tiles_i))
            step(nc.vector.tensor_copy(end[:, 0:1], n_tiles[:, 0:1]))
            for e in range(1, E):
                step(nc.vector.tensor_tensor(end[:, e:e + 1], end[:, e - 1:e], n_tiles[:, e:e + 1], ALU.add))
            step(nc.vector.tensor_scalar(skip, n_tiles, float(-P), float(REGION), ALU.mult, ALU.add))
            step(nc.vector.memset(expert_of, 0.0))
            step(nc.vector.tensor_scalar(row_of, tile_row_sb[:], float(P), None, ALU.mult))
            for e in range(E - 1):
                step(nc.vector.tensor_scalar(passed, tile_row_sb[:], end[:, e:e + 1], None, ALU.is_ge))
                step(nc.vector.tensor_tensor(expert_of, expert_of, passed, ALU.add))
                step(nc.vector.scalar_tensor_tensor(row_of, passed, skip[:, e:e + 1], row_of, ALU.mult, ALU.add))
            last = jump[:, 0:1]
            step(nc.vector.tensor_scalar(last, n_tiles[:, E - 1:E], -1.0, 0.0, ALU.add, ALU.max))
            step(nc.vector.tensor_scalar(last, last, float(P), float((E - 1) * REGION), ALU.mult, ALU.add))
            step(nc.vector.tensor_scalar(row_of, row_of, last, None, ALU.min))
            step(nc.vector.tensor_copy(plan_i[:, 0], expert_of))
            nc.vector.tensor_copy(plan_i[:, 1], row_of).then_inc(plan_out, 1)

            step(nc.vector.tensor_scalar(skip, skip, -1.0, None, ALU.mult))
            for e in range(E - 1):
                step(nc.vector.tensor_scalar(behind[:], experts[:], float(e), None, ALU.is_gt))
                step(nc.vector.scalar_tensor_tensor(slots[:], behind[:], skip[:, e:e + 1], slots[:],
                                                    ALU.mult, ALU.add))
            nc.vector.tensor_copy(packed[:], slots[:]).then_inc(packed_out, 1)

            tv = tops[:].rearrange("p t k -> p k t")
            nc.vector.tensor_tensor(weight[:, 1], tv[:, 1], tv[:, 0], ALU.subtract).then_inc(weight_exp, 1)
            dve.wait_ge(weight_exp, 2)
            nc.vector.tensor_scalar(weight[:, 0], weight[:, 1], 1.0, None, ALU.add).then_inc(weight_out, 1)
            dve.wait_ge(weight_out, 1)
            nc.vector.reciprocal(weight[:, 0], weight[:, 0]).then_inc(weight_out, 1)
            dve.wait_ge(weight_out, 2)
            nc.vector.tensor_tensor(weight[:, 1], weight[:, 1], weight[:, 0], ALU.mult).then_inc(weight_out, 1)

            def copy_xe(t):
                dve.wait_ge(xet_done, t + 1)
                nc.vector.tensor_copy(xe_t[:], bank[2][:, 0:C * P].rearrange("p (c n) -> p c n", c=C))\
                    .then_inc(xet_out, 1)

            def hidden_rows(t):
                dve.wait_ge(sig_out, t + 1)
                nc.vector.tensor_tensor(gate, bank[0][:], gate, ALU.mult).then_inc(hid_step, 1)
                dve.wait_ge(hid_step, t + 1)
                dve.wait_ge(gv_done, t + 1)
                if not first(t):
                    dve.wait_ge(ht_done, t)
                nc.vector.tensor_tensor(hid, bank[1][:], gate, ALU.mult).then_inc(hid_out, 1)

            def copy_y(t):
                dve.wait_ge(y_done, t + 1)
                if not first(t):
                    dve.wait_ge(ye_stored, 16 * t)
                nc.vector.tensor_copy(ye, bank[4][:, 0:D]).then_inc(ye_out, 1)

            copy_xe(0)
            hidden_rows(0)
            copy_xe(1)
            with dve.Fori(1, MOE_TILES - 1) as t:
                hidden_rows(t)
                copy_xe(t + 1)
                copy_y(t - 1)
            hidden_rows(MOE_TILES - 1)
            copy_y(MOE_TILES - 2)
            copy_y(MOE_TILES - 1)

            def combine(t, r, s):
                dve.wait_ge(picked[s], 32 * (r + 1))
                dve.wait_ge(back_in[s], 16 * (r + 1))
                if not first(r):
                    dve.wait_ge(stored[s], 16 * r)
                nc.vector.scalar_tensor_tensor(y_out[:, s], y_pick[:, s, 0], weight[:, 0, bass.ds(t, 1)],
                                               x2_back[:, s], ALU.mult, ALU.add).then_inc(sum_step, 1)
                dve.wait_ge(sum_step, t + 1)
                nc.vector.scalar_tensor_tensor(y_out[:, s], y_pick[:, s, 1], weight[:, 1, bass.ds(t, 1)],
                                               y_out[:, s], ALU.mult, ALU.add).then_inc(sum_out, 1)

            dve.wait_ge(weight_out, 3)
            for s in range(2):
                combine(s, 0, s)
            with dve.Fori(1, TILES // 2) as r:
                for s in range(2):
                    combine(2 * r + s, r, s)

        @block.tensor
        def _(pe):
            mm, tr = nc.tensor.matmul, nc.tensor.transpose
            pe.wait_ge(consts_in, CONSTS)

            def transposed(dst, src, sem_):
                for c in range(C):
                    last = tr(dst[:, c * P:(c + 1) * P], src[:, c * P:(c + 1) * P], ident_sb[:])
                last.then_inc(sem_, 1)

            def project(t, b, k):
                n = (t * BT + b) * 3 + k
                if k == 0:
                    pe.wait_ge(ctx_in[b], 16 * (t + 1))
                if not (isinstance(t, int) and n < 2):
                    pe.wait_ge(proj_out, n - 1)
                dst = proj_ps[(b * 3 + k) % 2]
                if k < 2:
                    for d in range(C):
                        last = mm(dst[:, 0:M], w_sb[:, WK1, d, k * P:(k + 1) * P], ctx_sb[:, b, d],
                                  start=(d == 0), stop=(d == C - 1))
                else:
                    for m in range(2):
                        for d in range(C):
                            last = mm(dst[:, m * D:(m + 1) * D], ctx_sb[:, b, d, m * P:(m + 1) * P],
                                      w_sb[:, WV1, d], start=(d == 0), stop=(d == C - 1))
                last.then_inc(proj_done, 1)

            def scores(t, u):
                b, g = u // G, u % G
                n = t * UNITS + u
                if g == 0:
                    pe.wait_ge(heads_done, t * BT + b + 1)
                    pe.wait_ge(proj_out, (t * BT + b) * 3 + 2)
                if not (isinstance(t, int) and n < 2):
                    pe.wait_ge(exp_done, n - 1)
                c, half = g // 2, g % 2
                q = q_heads[:, b % 2, c, half * JH:(half + 1) * JH].rearrange("p j n -> p (j n)")
                mm(score_ps[u % 2][:, 0:M], q, k_t[:, b % 2, c], start=True, stop=True).then_inc(score_done, 1)

            def transpose_probs(t, u):
                n = t * UNITS + u
                pe.wait_ge(exp_done, n + 1)
                if not (isinstance(t, int) and n < 1):
                    pe.wait_ge(pt_out, n)
                for m in range(2):
                    last = tr(pt_ps[:, m * P:(m + 1) * P], prob[:, u % P_SLOTS, m * P:(m + 1) * P], ident_sb[:])
                last.then_inc(pt_done, 1)

            def values(t, u):
                b, g = u // G, u % G
                n = t * UNITS + u
                pe.wait_ge(pt_out, n + 1)
                if g == 0:
                    pe.wait_ge(proj_out, (t * BT + b) * 3 + 3)
                    if not (isinstance(t, int) and t * BT + b < 1):
                        pe.wait_ge(o_out, t * BT + b)
                c, half = g // 2, g % 2
                for m in range(2):
                    last = mm(o_ps[64 * half:64 * half + 64, c * P:(c + 1) * P],
                              v_sb[:, b % 2, m, g * 64:(g + 1) * 64], prob_t[:, u % 2, m],
                              start=(m == 0), stop=(m == 1))
                last.then_inc(pv_done, 1)

            def query(t):
                pe.wait_ge(xt_out[0], t + 1)
                for c in range(C):
                    for d in range(C):
                        last = mm(f_ps[:, c * P:(c + 1) * P], w_sb[:, WQ1, d, c * P:(c + 1) * P], xn1_t[:, d],
                                  start=(d == 0), stop=(d == C - 1))
                last.then_inc(q_done, 1)

            for c in range(C):
                for d in range(C):
                    last = mm(f_ps[:, c * B:(c + 1) * B], w_sb[:, WV1, d, c * P:(c + 1) * P], tail_sb[:, d],
                              start=(d == 0), stop=(d == C - 1))
            last.then_inc(tail_done, 1)
            pe.wait_ge(tail_out, 1)
            pe.wait_ge(ln_out[0], 1)
            transposed(f_ps, xn1, xt_done[0])
            query(0)
            for k in range(3):
                project(0, 0, k)

            def body(i):
                att, nxt, rest, route = phases(i)
                for u in range(UNITS):
                    b, g = u // G, u % G
                    if att:
                        scores(i, u)
                        if g < 3 and b < 3:
                            project(i, b + 1, g)
                        elif g < 3 and nxt:
                            project(i + 1, 0, g)
                    if att and u >= 2:
                        values(i, u - 2)
                    if rest and u < 2:
                        values(i - 1, UNITS - 2 + u)
                    if att and u >= 1:
                        transpose_probs(i, u - 1)
                    if rest and u == 0:
                        transpose_probs(i - 1, UNITS - 1)
                    if route and u == 0:
                        r = i - 2
                        pe.wait_ge(xt_out[2], r + 1)
                        if not (isinstance(i, int) and i >= TILES):
                            pe.wait_ge(q_out, i + 1)
                        for d in range(C):
                            last = mm(f_ps[:, 0:E], xn3_t[:, d], wg_sb[:, d], start=(d == 0), stop=(d == C - 1))
                        last.then_inc(lg_done, 1)
                    if route and u == 1:
                        pe.wait_ge(any_out, i - 1)
                        for k in range(2):
                            last = mm(f_ps[:, k * E:(k + 1) * E], tri_sb[:, k], chosen_any[:], start=True, stop=True)
                        last.then_inc(rank_done, 1)
                    if rest and u == 1:
                        t = i - 1
                        pe.wait_ge(stats_done, t + 1)
                        if not first(t):
                            pe.wait_ge(xt_out[2], t)
                        for c in range(C):
                            for half in range(2):
                                last = mm(c_ps[:, c * 2 * P:(c + 1) * 2 * P], expand_sb[:, half],
                                          stat_rows[:, 2 * c + half].rearrange("p w n -> p (w n)"),
                                          start=(half == 0), stop=(half == 1))
                        last.then_inc(ex_done, 1)
                    if rest and u == 3:
                        pe.wait_ge(norm_out, i)
                        for c in range(C):
                            last = mm(c_ps[:, 0:D], o_norm[:, c], w_sb[:, WO1, c], start=(c == 0), stop=(c == C - 1))
                        last.then_inc(wo1_done, 1)
                    if nxt and u == 5:
                        pe.wait_ge(ln_out[0], i + 2)
                        if route:
                            pe.wait_ge(rank_step, (i - 1) * 4)
                        transposed(f_ps, xn1, xt_done[0])
                    if rest and u == 5:
                        pe.wait_ge(ln_out[1], i)
                        transposed(c_ps, xn2, xt_done[1])
                    if rest and u == 6:
                        t = i - 1
                        pe.wait_ge(xt_out[1], t + 1)
                        for k in range(4):
                            w, c = (WQ2, WK2)[k // C], k % C
                            for d in range(C):
                                last = mm(c_ps[:, k * P:(k + 1) * P], w_sb[:, w, d, c * P:(c + 1) * P], xn2_t[:, d],
                                          start=(d == 0), stop=(d == C - 1))
                        last.then_inc(qk_done, 1)
                        if nxt:
                            pe.wait_ge(xt_out[0], i + 2)
                        for d in range(C):
                            last = mm(f_ps[:, 0:D], xn2_t[:, d], w_sb[:, WV2, d], start=(d == 0), stop=(d == C - 1))
                        last.then_inc(v2_done, 1)
                    if rest and u in (9, 10):
                        t = i - 1
                        if u == 9:
                            pe.wait_ge(phiq_out, t + 1)
                            pe.wait_ge(v2_out, t + 1)
                        for g2 in (2 * (u - 9), 2 * (u - 9) + 1):
                            if g2 >= 2:
                                pe.wait_ge(sc2_out, t * G + g2 - 1)
                            c, half = g2 // 2, g2 % 2
                            mm((c_ps, f_ps)[g2 % 2][:], qk_phi[:, C + c],
                               phi_heads[:, c, half * JH:(half + 1) * JH].rearrange("p j n -> p (j n)"),
                               start=True, stop=True).then_inc(sc2_done, 1)
                    if rest and u == 11:
                        pe.wait_ge(sc2_out, i * G)
                        for h in range(H):
                            last = mm(c_ps[:, h * (HD + 1):(h + 1) * (HD + 1)], a_t[:, h], v_aug[:, h],
                                      start=True, stop=True)
                        last.then_inc(av_done, 1)
                    if rest and u == 12:
                        pe.wait_ge(merged_out, i)
                        transposed(c_ps, merged[:].rearrange("p h d -> p (h d)"), mt_done)
                    if nxt and u == 13:
                        if rest:
                            pe.wait_ge(sc2_out, i * G)
                        query(i + 1)
                    if rest and u == 13:
                        pe.wait_ge(mt_out, i)
                        for c in range(C):
                            last = mm(c_ps[:, 0:D], merged_t[:, c], w_sb[:, WO2, c], start=(c == 0), stop=(c == C - 1))
                        last.then_inc(wo2_done, 1)
                    if rest and u == 15:
                        pe.wait_ge(ln_out[2], i)
                        transposed(c_ps, xn3, xt_done[2])
            iterations(pe, body)

            pe.wait_ge(experts_in, EXPERTS)
            pe.wait_ge(plan_out, 1)

            def transpose_x(t):
                pe.wait_ge(xe_in, 16 * (t + 1))
                transposed(bank[2], xe, xet_done)

            def up(t):
                e = pe.value_load(plan_i[0:1, 0, bass.ds(t, 1)], min_val=0, max_val=E - 1)
                pe.wait_ge(xet_out, t + 1)
                for w, dst, done in ((w1_sb, bank[0], u_done), (w2_sb, bank[1], gv_done)):
                    if not first(t):
                        pe.wait_ge(hid_step if done is u_done else hid_out, t)
                    for d in range(C):
                        last = mm(dst[:], xe_t[:, d], w[:, bass.ds(e, 1), d].rearrange("p a f -> p (a f)"),
                                  start=(d == 0), stop=(d == C - 1))
                    last.then_inc(done, 1)

            def transpose_h(t):
                pe.wait_ge(hid_out, t + 1)
                for c in range(FC):
                    last = tr(bank[3][:, c * P:(c + 1) * P], hid[:, c * P:(c + 1) * P], ident_sb[:])
                last.then_inc(ht_done, 1)

            def down(t):
                e = pe.value_load(plan_i[0:1, 0, bass.ds(t, 1)], min_val=0, max_val=E - 1)
                pe.wait_ge(ht_out, t + 1)
                if not first(t):
                    pe.wait_ge(ye_out, t)
                for c in range(FC):
                    last = mm(bank[4][:, 0:D], hid_t[:, c], w3_sb[:, bass.ds(e, 1), c].rearrange("p a d -> p (a d)"),
                              start=(c == 0), stop=(c == FC - 1))
                last.then_inc(y_done, 1)

            transpose_x(0)
            up(0)
            transpose_x(1)
            transpose_h(0)
            with pe.Fori(1, MOE_TILES - 1) as t:
                up(t)
                transpose_x(t + 1)
                down(t - 1)
                transpose_h(t)
            up(MOE_TILES - 1)
            down(MOE_TILES - 2)
            transpose_h(MOE_TILES - 1)
            down(MOE_TILES - 1)


def kernel(x, ctx_1024, L0_xattn_wq, L0_xattn_wk, L0_xattn_wv, L0_xattn_wo, L0_xattn_bo, L0_attn_mask,
           L0_attn_Wq, L0_attn_bq, L0_attn_Wk, L0_attn_bk, L0_attn_Wv, L0_attn_bv, L0_attn_Wo, L0_attn_bo,
           L0_ffn_Wg, L0_ffn_W1, L0_ffn_W2, L0_ffn_W3):
    import numpy as np
    import concourse.bacc as bacc
    from concourse.bass_utils import run_bass_kernel_spmd as run

    def lay(a):
        return np.ascontiguousarray(a)

    ctx = np.asarray(ctx_1024)
    rows = np.arange(P)
    head_of = (rows % 64) // HD
    half_of = rows // 64
    arrays = {
        "x": lay(np.asarray(x).reshape(TILES, P, D)),
        "ctx_t": lay(ctx.reshape(TILES, BT, M, C, P).transpose(0, 1, 4, 3, 2)),
        "tail_t": lay(ctx[:, M - 1].reshape(B, C, P).transpose(2, 1, 0)),
        "w_attn": lay(np.stack([np.asarray(w).T.reshape(C, P, D).transpose(1, 0, 2) for w in (
            L0_xattn_wq, L0_xattn_wk, L0_xattn_wv, L0_xattn_wo,
            L0_attn_Wq, L0_attn_Wk, L0_attn_Wv, L0_attn_Wo)], axis=1)),
        "bias_rows": lay(np.stack([np.asarray(v) for v in (L0_xattn_bo, L0_attn_bv, L0_attn_bo)])),
        "bias_qk": lay(np.stack([np.asarray(L0_attn_bq).reshape(C, P), np.asarray(L0_attn_bk).reshape(C, P)])
                       .reshape(2 * C, P).T),
        "wg": lay(np.asarray(L0_ffn_Wg).reshape(C, P, E).transpose(1, 0, 2)),
        "w1": lay(np.asarray(L0_ffn_W1).reshape(E, C, P, F).transpose(2, 0, 1, 3)),
        "w2": lay(np.asarray(L0_ffn_W2).reshape(E, C, P, F).transpose(2, 0, 1, 3)),
        "w3": lay(np.asarray(L0_ffn_W3).reshape(E, FC, P, D).transpose(2, 0, 1, 3)),
        "ident": np.eye(P, dtype=np.float32),
        "head_mask": lay((half_of[:, None] * JH + head_of[:, None] == np.arange(2 * JH)[None]).astype(np.float32)),
        "fold_mask": lay((head_of[:, None] == np.arange(JH)[None]).astype(np.float32)),
        "causal": lay(((rows[:, None] // NQ == rows[None] // NQ) & (rows[:, None] <= rows[None])).astype(np.float32)),
        "tri": lay(np.stack([rows[:, None] < rows[None], rows[:, None] >= 0 * rows[None]], axis=1).astype(np.float32)),
        "expand": lay(np.stack([(half_of[None] == half) & (rows[:, None] // NQ == head_of[None])
                                for half in range(2)], axis=1).astype(np.float32)),
        "query_eye": lay((rows[:, None] % NQ == np.arange(NQ)[None]).astype(np.float32)),
        "expert_row": lay(np.broadcast_to(np.stack([np.arange(E), np.arange(E) * REGION])[None],
                                          (P, 2, E)).astype(np.float32)),
        "tile_row": lay(np.broadcast_to(np.arange(MOE_TILES, dtype=np.float32)[None], (P, MOE_TILES))),
    }
    nc = bacc.Bacc("TRN2", target_bir_lowering=False, num_devices=1)
    aps = {k: nc.dram_tensor(k, v.shape, mybir.dt.from_np(v.dtype), kind="ExternalInput").ap()
           for k, v in arrays.items()}
    f32 = mybir.dt.float32
    routed = nc.dram_tensor("routed", (E * REGION, D), f32, kind="Internal").ap()
    hidden = nc.dram_tensor("hidden", (MOE_TILES * P, D), f32, kind="Internal").ap()
    x2_dram = nc.dram_tensor("x2_dram", (TILES, P, D), f32, kind="Internal").ap()
    out = nc.dram_tensor("out", (TILES, P, D), f32, kind="ExternalOutput").ap()
    perceiver(nc, **aps, routed=routed, hidden=hidden, x2_dram=x2_dram, out=out)
    got = run(nc, [arrays], core_ids=[0])
    return got.results[0]["out"].reshape(B, NQ, D)
```

```python
from contextlib import ExitStack

import concourse.bass as bass
from concourse import mybir

B, NQ, D = 128, 32, 256
M = 257
H, HD = 16, 16
E, F = 8, 512
P = 128
TOK = B * NQ
TILES = TOK // P
BT = P // NQ
C = D // P
G = 4
JH = H // G
UNITS = BT * G
FC = F // P
REGION = TOK + P
TOPK = 2
MOE_TILES = TOPK * TOK // P + E - 1
LN_EPS = 1e-5
ATT_EPS = 1e-6
WQ1, WK1, WV1, WO1, WQ2, WK2, WV2, WO2 = range(8)
P_SLOTS = 8


def first(t):
    return isinstance(t, int) and t == 0


def perceiver(nc, x, ctx_t, tail_t, w_attn, bias_rows, bias_qk, wg, w_expert,
              ident, head_mask, fold_mask, causal, tri, expand, query_eye, expert_row, tile_row,
              routed, hidden, x2_dram, out):
    f32 = mybir.dt.float32
    i32 = mybir.dt.int32
    u32 = mybir.dt.uint32
    ACT = mybir.ActivationFunctionType
    ALU = mybir.AluOpType
    AX = mybir.AxisListType.X

    with ExitStack() as stack:
        def sb(name, shape, dt=f32):
            return stack.enter_context(nc.sbuf_tensor(name, shape, dt))

        def sem(name):
            return stack.enter_context(nc.semaphore(name))

        ident_sb = sb("ident_sb", [P, P])
        head_mask_sb = sb("head_mask_sb", [P, 2 * JH])
        scaled_mask_sb = sb("scaled_mask_sb", [P, 2 * JH])
        fold_mask_sb = sb("fold_mask_sb", [P, JH])
        causal_sb = sb("causal_sb", [P, P])
        tri_sb = sb("tri_sb", [P, 2, P])
        expand_sb = sb("expand_sb", [P, 2, P])
        query_eye_sb = sb("query_eye_sb", [P, NQ])
        expert_row_sb = sb("expert_row_sb", [P, 2, E])
        tile_row_sb = sb("tile_row_sb", [P, MOE_TILES])
        w_sb = sb("w_sb", [P, 8, C, D])
        bias_sb = sb("bias_sb", [P, 3, D])
        bias_qk_sb = sb("bias_qk_sb", [P, 4])
        wg_sb = sb("wg_sb", [P, C, E])
        expert_sb = sb("expert_sb", [P, 3, E, C * F])
        w1_sb = expert_sb[:, 0].rearrange("p e (c f) -> p e c f", c=C)
        w2_sb = expert_sb[:, 1].rearrange("p e (c f) -> p e c f", c=C)
        w3_sb = expert_sb[:, 2].rearrange("p e (c d) -> p e c d", c=FC)
        neg_half = sb("neg_half", [P, 1])
        tail_sb = sb("tail_sb", [P, C, B])
        v_tail = sb("v_tail", [P, C, B])

        ctx_sb = sb("ctx_sb", [P, BT, C, M])
        k_t = sb("k_t", [P, 2, C, M])
        v_sb = sb("v_sb", [P, 2, 2, D])
        x_ln1 = sb("x_ln1", [P, D])
        xn1 = sb("xn1", [P, D])
        xn1_t = sb("xn1_t", [P, C, P])
        q_t = sb("q_t", [P, C, P])
        q_heads = sb("q_heads", [P, 2, C, 2 * JH, NQ])
        neg_max = sb("neg_max", [P, UNITS])
        prob = sb("prob", [P, P_SLOTS, M])
        row_stat = sb("row_stat", [P, G, 2, BT])
        prob_t = sb("prob_t", [P, 2, 2, P])
        o_masked = sb("o_masked", [P, C, JH, NQ])
        o_t = sb("o_t", [P, C, BT, NQ])
        stat_rows = sb("stat_rows", [P, G, 2 * BT, NQ])
        recip_sum = sb("recip_sum", [P, C, P])
        o_tail = sb("o_tail", [P, C, P])
        o_norm = sb("o_norm", [P, C, P])

        x_res = sb("x_res", [P, D])
        x1 = sb("x1", [P, D])
        xn2 = sb("xn2", [P, D])
        xn2_t = sb("xn2_t", [P, C, P])
        qk_pre = sb("qk_pre", [P, 4, P])
        qk_min = sb("qk_min", [P, 4, P])
        qk_phi = sb("qk_phi", [P, 4, P])
        v_aug = sb("v_aug", [P, H, HD + 1])
        phi_heads = sb("phi_heads", [P, C, 2 * JH, P])
        a_t = sb("a_t", [P, H, P])
        den = sb("den", [P, H])
        merged = sb("merged", [P, H, HD])
        merged_t = sb("merged_t", [P, C, P])
        x2 = sb("x2", [P, D])
        xn3 = sb("xn3", [P, D])
        xn3_t = sb("xn3_t", [P, C, P])
        ln = [sb(f"ln{k}", [P, 16]) for k in range(3)]

        logits = sb("logits", [P, E])
        top = sb("top", [P, E])
        top_at = sb("top_at", [P, E], u32)
        top_f = sb("top_f", [P, TOPK])
        chosen = sb("chosen", [P, TOPK, E])
        chosen_any = sb("chosen_any", [P, E])
        row_next = sb("row_next", [P, E])
        pos = sb("pos", [P, E])
        pos_chosen = sb("pos_chosen", [P, TOPK, E])
        slot_f = sb("slot_f", [P, TOPK])
        slot = sb("slot", [P, TOPK], i32)
        slots = sb("slots", [P, TILES, TOPK])
        experts = sb("experts", [P, TILES, TOPK])
        behind = sb("behind", [P, TILES, TOPK])
        packed = sb("packed", [P, TILES, TOPK], i32)
        pick_at = sb("pick_at", [P, 2, TOPK], i32)
        tops = sb("tops", [P, TILES, TOPK])
        plan = sb("plan", [P, 8, MOE_TILES])
        plan_i = sb("plan_i", [P, 3, MOE_TILES], i32)
        weight = sb("weight", [P, TOPK, TILES])

        zeros = sb("zeros", [P, D])
        xe = sb("xe", [P, D])
        xe_t = sb("xe_t", [P, C, P])
        spare_a = phi_heads[:].rearrange("p c j n -> p (c j n)")
        spare_b = a_t[:].rearrange("p h n -> p (h n)")
        gate, hid = spare_a[:, 0:F], spare_a[:, F:2 * F]
        hid_t = spare_a[:, 2 * F:3 * F].rearrange("p (c n) -> p c n", c=FC)
        ye = spare_a[:, 3 * F:3 * F + D]
        y_pick = spare_b[:, 0:4 * D].rearrange("p (s r d) -> p s r d", s=2, r=TOPK)
        x2_back = spare_b[:, 4 * D:6 * D].rearrange("p (s d) -> p s d", s=2)
        y_out = spare_b[:, 6 * D:8 * D].rearrange("p (s d) -> p s d", s=2)

        bank = [stack.enter_context(nc.psum_tensor(f"bank{k}", [P, 512], f32)) for k in range(8)]
        proj_ps = bank[0:2]
        score_ps = bank[2:4]
        pt_ps, o_ps, c_ps, f_ps = bank[4:8]

        consts_in = sem("consts_in")
        experts_in = sem("experts_in")
        tail_done, tail_out = sem("tail_done"), sem("tail_out")
        ctx_in = [sem(f"ctx_in{b}") for b in range(BT)]
        xln_in, xres_in = sem("xln_in"), sem("xres_in")
        proj_done, proj_out = sem("proj_done"), sem("proj_out")
        score_done, max_done, exp_done = sem("score_done"), sem("max_done"), sem("exp_done")
        pt_done, pt_out, pv_done, o_out = sem("pt_done"), sem("pt_out"), sem("pv_done"), sem("o_out")
        o_step = sem("o_step")
        heads_done = sem("heads_done")
        sums_inverted = sem("sums_inverted")
        last_copied, stats_done = sem("last_copied"), sem("stats_done")
        ln_step = [sem(f"ln_step{k}") for k in range(3)]
        ln_var = [sem(f"ln_var{k}") for k in range(3)]
        ln_eps_done = [sem(f"ln_eps_done{k}") for k in range(3)]
        ln_rstd = [sem(f"ln_rstd{k}") for k in range(3)]
        ln_out = [sem(f"ln_out{k}") for k in range(3)]
        xt_done = [sem(f"xt_done{k}") for k in range(3)]
        xt_out = [sem(f"xt_out{k}") for k in range(3)]
        q_done, q_out = sem("q_done"), sem("q_out")
        ex_done, ex_step, norm_out = sem("ex_done"), sem("ex_step"), sem("norm_out")
        wo1_done, xb_done, x1_out, x1b_done = sem("wo1_done"), sem("xb_done"), sem("x1_out"), sem("x1b_done")
        qk_done, v2_done, v2_out = sem("qk_done"), sem("v2_done"), sem("v2_out")
        qkb_step, qkb_out, qke_out, phi_out, phiq_out = (sem("qkb_step"), sem("qkb_out"), sem("qke_out"),
                                                         sem("phi_out"), sem("phiq_out"))
        sc2_done, sc2_out = sem("sc2_done"), sem("sc2_out")
        av_done, av_step, merged_out = sem("av_done"), sem("av_step"), sem("merged_out")
        mt_done, mt_out = sem("mt_done"), sem("mt_out")
        wo2_done, x2_out, x2_stored = sem("wo2_done"), sem("x2_out"), sem("x2_stored")
        lg_done, lg_step, any_out, rank_done, rank_step, slot_out = (
            sem("lg_done"), sem("lg_step"), sem("any_out"), sem("rank_done"), sem("rank_step"), sem("slot_out"))
        routed_out = sem("routed_out")
        setup = sem("setup")
        packed_out = sem("packed_out")
        plan_step, plan_out, zero_in = sem("plan_step"), sem("plan_out"), sem("zero_in")
        weight_exp, weight_out = sem("weight_exp"), sem("weight_out")
        xe_in, xet_done, xet_out = sem("xe_in"), sem("xet_done"), sem("xet_out")
        u_done, gv_done, sig_out, hid_step, hid_out = (sem("u_done"), sem("gv_done"), sem("sig_out"),
                                                       sem("hid_step"), sem("hid_out"))
        ht_done, ht_out, y_done, ye_out, ye_stored = (sem("ht_done"), sem("ht_out"), sem("y_done"),
                                                      sem("ye_out"), sem("ye_stored"))
        pick_ready = sem("pick_ready")
        waits_passed = sem("waits_passed")
        picked = [sem(f"picked{s}") for s in range(2)]
        back_in = [sem(f"back_in{s}") for s in range(2)]
        sum_step, sum_out = sem("sum_step"), sem("sum_out")
        stored = [sem(f"stored{s}") for s in range(2)]
        CONSTS = 16 * 17
        EXPERTS = 16 * 3 * E

        block = stack.enter_context(nc.Block())

        def phases(i):
            if not isinstance(i, int):
                return True, True, True, True
            return i < TILES, i + 1 < TILES, 1 <= i <= TILES, 2 <= i <= TILES + 1

        def apart(engine):
            engine.sem_inc(waits_passed, 1)

        def iterations(engine, body):
            for i in range(3):
                body(i)
            with engine.Fori(3, TILES - 1) as i:
                body(i)
            for i in range(TILES - 1, TILES + 2):
                body(i)

        @block.sync
        def _(sp):
            def load_ctx(t, b):
                if not first(t):
                    sp.wait_ge(proj_done, ((t - 1) * BT + b + 1) * 3)
                sp.dma_start(ctx_sb[:, b], ctx_t[t, b]).then_inc(ctx_in[b], 16)

            def load_xln(t):
                if not first(t):
                    sp.wait_ge(ln_out[0], t)
                sp.dma_start(x_ln1[:], x[t]).then_inc(xln_in, 16)

            def load_xres(t):
                if not first(t):
                    sp.wait_ge(x1_out, t)
                sp.dma_start(x_res[:], x[t]).then_inc(xres_in, 16)

            sp.dma_start(w_sb[:], w_attn).then_inc(consts_in, 16)
            load_xln(0)
            for b in range(BT):
                load_ctx(0, b)
            sp.dma_start(tail_sb[:], tail_t).then_inc(consts_in, 16)
            for k in range(3):
                sp.dma_start(bias_sb[:, k], bias_rows[k:k + 1, :].broadcast_to([P, D])).then_inc(consts_in, 16)
            load_xres(0)

            def body(i):
                att, nxt, rest, late = phases(i)
                if nxt:
                    load_xln(i + 1)
                if nxt:
                    for b in range(BT):
                        load_ctx(i + 1, b)
                if rest and nxt:
                    load_xres(i)
                if isinstance(i, int) and i == TILES - 1:
                    load_xres(i)
                if late:
                    sp.wait_ge(x2_out, i - 1)
                    sp.dma_start(x2_dram[i - 2], x2[:]).then_inc(x2_stored, 16)

            def load_expert(k):
                dst = expert_sb[:].rearrange("p w e n -> p (w e) n")
                if isinstance(k, int):
                    sp.dma_start(dst[:, k], w_expert[k]).then_inc(experts_in, 16)
                else:
                    sp.dma_start(dst[:, bass.ds(k, 1)].rearrange("p a n -> p (a n)"),
                                 w_expert[bass.ds(k, 1)].rearrange("a p n -> p (a n)")).then_inc(experts_in, 16)

            for i in range(3):
                body(i)
            with sp.Fori(3, 3 + 3 * E) as i:
                body(i)
                load_expert(i - 3)
            with sp.Fori(3 + 3 * E, TILES - 1) as i:
                body(i)
            for i in range(TILES - 1, TILES + 2):
                body(i)

            sp.wait_ge(plan_out, 1)
            sp.wait_ge(routed_out, 32 * TILES)
            for e in range(E):
                row = sp.value_load(plan_i[0:1, 2, e:e + 1], min_val=0, max_val=E * REGION - P)
                sp.dma_start(routed[bass.ds(row, P), :], zeros[:]).then_inc(zero_in, 16)
            sp.wait_ge(zero_in, 16 * E)

            def load_tile(t):
                if not first(t):
                    sp.wait_ge(xet_done, t)
                row = sp.value_load(plan_i[0:1, 1, bass.ds(t, 1)], min_val=0, max_val=E * REGION - P)
                sp.dma_start(xe[:], routed[bass.ds(row, P), :]).then_inc(xe_in, 16)

            load_tile(0)
            with sp.Fori(1, MOE_TILES) as t:
                load_tile(t)

            def load_back(t, s):
                if not (isinstance(t, int) and t < 2):
                    sp.wait_ge(sum_out, t - 1)
                sp.dma_start(x2_back[:, s], x2_dram[t]).then_inc(back_in[s], 16)

            sp.wait_ge(x2_stored, 16 * TILES)
            for s in range(2):
                load_back(s, s)
            with sp.Fori(1, TILES // 2) as r:
                for s in range(2):
                    load_back(2 * r + s, s)

        @block.scalar
        def _(act):
            for dst, src in ((ident_sb[:], ident), (head_mask_sb[:], head_mask),
                             (fold_mask_sb[:], fold_mask), (causal_sb[:], causal), (tri_sb[:], tri),
                             (expand_sb[:], expand), (query_eye_sb[:], query_eye),
                             (expert_row_sb[:], expert_row), (tile_row_sb[:], tile_row),
                             (bias_qk_sb[:], bias_qk), (wg_sb[:], wg)):
                act.dma_start(dst, src).then_inc(consts_in, 16)
            act.dma_start(scaled_mask_sb[:], head_mask).then_inc(consts_in, 16)
            act.wait_ge(tail_done, 1)
            nc.scalar.copy(v_tail[:], f_ps[:, 0:C * B].rearrange("p (c b) -> p c b", c=C)).then_inc(tail_out, 1)

            def copy_proj(t, b, k):
                n = (t * BT + b) * 3 + k
                bank_of = proj_ps[(b * 3 + k) % 2]
                act.wait_ge(proj_done, n + 1)
                if k < 2:
                    nc.scalar.copy(k_t[:, b % 2, k], bank_of[:, 0:M]).then_inc(proj_out, 1)
                else:
                    nc.scalar.copy(v_sb[:, b % 2], bank_of[:].rearrange("p (m d) -> p m d", m=2))\
                        .then_inc(proj_out, 1)

            def copy_xt(t, k, dst, src):
                act.wait_ge(xt_done[k], t + 1)
                nc.scalar.copy(dst[:], src[:, 0:C * P].rearrange("p (c n) -> p c n", c=C)).then_inc(xt_out[k], 1)

            def copy_q(t):
                act.wait_ge(q_done, t + 1)
                if not first(t):
                    act.wait_ge(heads_done, t * BT)
                nc.scalar.copy(q_t[:], f_ps[:, 0:C * P].rearrange("p (c n) -> p c n", c=C)).then_inc(q_out, 1)

            def exponentials(t, u):
                b, g = u // G, u % G
                n = t * UNITS + u
                act.wait_ge(max_done, n + 1)
                if not (isinstance(t, int) and n < P_SLOTS):
                    act.wait_ge(pt_done, n - P_SLOTS + 1)
                    if g == 0:
                        act.wait_ge(last_copied, t * BT + b - 1)
                if u == 0 and not first(t):
                    act.wait_ge(stats_done, t)
                nc.scalar.activation(prob[:, u % P_SLOTS], score_ps[u % 2][:, 0:M], ACT.Exp,
                                     bias=neg_max[:, u:u + 1], scale=1.0,
                                     accum_out=row_stat[:, g, 0, b:b + 1]).then_inc(exp_done, 1)

            copy_xt(0, 0, xn1_t, f_ps)
            copy_q(0)
            for k in range(3):
                copy_proj(0, 0, k)

            def body(i):
                att, nxt, rest, late = phases(i)
                for u in range(UNITS):
                    b, g = u // G, u % G
                    if att:
                        exponentials(i, u)
                    if late and u == 2:
                        act.wait_ge(mt_done, i - 1)
                        nc.scalar.copy(merged_t[:], c_ps[:, 0:C * P].rearrange("p (c n) -> p c n", c=C))\
                            .then_inc(mt_out, 1)
                    if late and u == 5:
                        copy_xt(i - 2, 2, xn3_t, f_ps)
                    if rest and u == 8:
                        copy_xt(i - 1, 1, xn2_t, c_ps)
                    if nxt and u == 10:
                        copy_xt(i + 1, 0, xn1_t, f_ps)
                    if nxt and u == 13:
                        copy_q(i + 1)
                    if att and g < 3 and b < 3:
                        copy_proj(i, b + 1, g)
                    elif att and g < 3 and nxt:
                        copy_proj(i + 1, 0, g)
                    if rest and u == 9:
                        act.wait_ge(qkb_out, i)
                        nc.scalar.activation(qk_min[:], qk_min[:], ACT.Exp).then_inc(qke_out, 1)
            iterations(act, body)

            act.wait_ge(weight_exp, 1)
            nc.scalar.activation(weight[:, 1], weight[:, 1], ACT.Exp).then_inc(weight_exp, 1)

            def expert_tile(t):
                act.wait_ge(u_done, t + 1)
                if not first(t):
                    act.wait_ge(hid_out, t)
                nc.scalar.activation(gate, bank[0][:], ACT.Sigmoid).then_inc(sig_out, 1)

            def copy_hid(t):
                act.wait_ge(ht_done, t + 1)
                nc.scalar.copy(hid_t, bank[3][:].rearrange("p (c n) -> p c n", c=FC)).then_inc(ht_out, 1)

            expert_tile(0)
            with act.Fori(1, MOE_TILES) as t:
                expert_tile(t)
                copy_hid(t - 1)
            copy_hid(MOE_TILES - 1)

            def store(t, s):
                act.wait_ge(sum_out, t + 1)
                act.dma_start(out[t], y_out[:, s]).then_inc(stored[s], 16)

            with act.Fori(0, TILES // 2) as r:
                for s in range(2):
                    store(2 * r + s, s)
            for s in range(2):
                act.wait_ge(stored[s], 16 * (TILES // 2))

        @block.gpsimd
        def _(pool):
            nc.gpsimd.memset(neg_half[:], -0.5).then_inc(setup, 1)
            nc.gpsimd.memset(zeros[:], 0.0).then_inc(setup, 1)
            nc.gpsimd.memset(v_aug[:], 1.0).then_inc(setup, 1)
            pool.wait_ge(setup, 3)
            pool.wait_ge(consts_in, CONSTS)
            nc.gpsimd.tensor_scalar(scaled_mask_sb[:], head_mask_sb[:], float(HD) ** -0.5, None, ALU.mult)\
                .then_inc(setup, 1)
            pool.wait_ge(setup, 4)

            def rstd(t, k):
                pool.wait_ge(ln_var[k], t + 1)
                apart(pool)
                nc.gpsimd.tensor_scalar(ln[k][:, 9:10], ln[k][:, 7:8], LN_EPS, None, ALU.add)\
                    .then_inc(ln_eps_done[k], 1)
                pool.wait_ge(ln_eps_done[k], t + 1)
                nc.gpsimd.tensor_tensor(ln[k][:, 8:9], ln[k][:, 9:10], neg_half[:], ALU.pow)\
                    .then_inc(ln_rstd[k], 1)

            def split_heads(t, b):
                n = t * BT + b
                pool.wait_ge(q_out, t + 1)
                if not (isinstance(t, int) and n < 2):
                    pool.wait_ge(score_done, (n - 1) * G)
                src = q_t[:, :, b * NQ:(b + 1) * NQ].unsqueeze(2).broadcast_to([P, C, 2 * JH, NQ])
                msk = scaled_mask_sb[:].unsqueeze(1).unsqueeze(3).broadcast_to([P, C, 2 * JH, NQ])
                nc.gpsimd.tensor_tensor(q_heads[:, b % 2], src, msk, ALU.mult).then_inc(heads_done, 1)

            def last_column(t, b):
                pool.wait_ge(exp_done, (t * BT + b + 1) * G)
                if b == 0 and not first(t):
                    pool.wait_ge(stats_done, t)
                s = (b * G) % P_SLOTS
                apart(pool)
                nc.gpsimd.tensor_copy(row_stat[:, :, 1, b], prob[:, s:s + G, M - 1]).then_inc(last_copied, 1)

            rstd(0, 0)
            split_heads(0, 0)

            def body(i):
                att, nxt, rest, late = phases(i)
                for u in range(UNITS):
                    b, g = u // G, u % G
                    if att and g == 1 and b < 3:
                        split_heads(i, b + 1)
                    if nxt and u == 15:
                        split_heads(i + 1, 0)
                    if att and g == 3 and b < 3:
                        last_column(i, b)
                    if rest and u == 0:
                        last_column(i - 1, 3)
                    if rest and u == 1:
                        pool.wait_ge(last_copied, i * BT)
                        pool.wait_ge(sums_inverted, i)
                        if not (isinstance(i, int) and i < 2):
                            pool.wait_ge(ex_done, i - 1)
                        src = row_stat[:].rearrange("p g w b -> p (g w b)").unsqueeze(2)\
                            .broadcast_to([P, G * 2 * BT, NQ])
                        eye = query_eye_sb[:].unsqueeze(1).broadcast_to([P, G * 2 * BT, NQ])
                        nc.gpsimd.tensor_tensor(stat_rows[:].rearrange("p g w n -> p (g w) n"), src, eye,
                                                ALU.mult).then_inc(stats_done, 1)
                    if rest and u == 2:
                        pool.wait_ge(xres_in, i * 16)
                        nc.gpsimd.tensor_tensor(x_res[:], x_res[:], bias_sb[:, 0], ALU.add).then_inc(xb_done, 1)
                    if late and u == 3:
                        rstd(i - 2, 2)
                    if nxt and u == 4:
                        rstd(i + 1, 0)
                    if rest and u == 6:
                        rstd(i - 1, 1)
                    if rest and u == 10:
                        pool.wait_ge(phi_out, i)
                        if not (isinstance(i, int) and i < 2):
                            pool.wait_ge(sc2_done, (i - 1) * G)
                        for c in range(C):
                            src = qk_phi[:, c].unsqueeze(1).broadcast_to([P, 2 * JH, P])
                            msk = head_mask_sb[:].unsqueeze(2).broadcast_to([P, 2 * JH, P])
                            nc.gpsimd.tensor_tensor(phi_heads[:, c], src, msk, ALU.mult).then_inc(phiq_out, 1)
                    if rest and u == 12:
                        pool.wait_ge(x1_out, i)
                        pool.wait_ge(ln_out[1], i)
                        nc.gpsimd.tensor_tensor(x1[:], x1[:], bias_sb[:, 2], ALU.add).then_inc(x1b_done, 1)
                    if late and u == 9:
                        pool.wait_ge(slot_out, i - 1)
                        for r in range(TOPK):
                            apart(pool)
                            pool.indirect_dma_start(
                                routed, bass.IndirectOffsetOnAxis(ap=slot[:, r:r + 1], axis=0), xn3[:], None)\
                                .then_inc(routed_out, 16)
            iterations(pool, body)

            def pick(t, s):
                if not (isinstance(t, int) and t < 2):
                    pool.wait_ge(sum_out, t - 1)
                apart(pool)
                nc.gpsimd.tensor_copy(pick_at[:, s], packed[:, bass.ds(t, 1)].rearrange("p a k -> p (a k)"))\
                    .then_inc(pick_ready, 1)
                pool.wait_ge(pick_ready, t + 1)
                for r in range(TOPK):
                    apart(pool)
                    pool.indirect_dma_start(
                        y_pick[:, s, r], None, hidden,
                        bass.IndirectOffsetOnAxis(ap=pick_at[:, s, r:r + 1], axis=0)).then_inc(picked[s], 16)

            def store_tile(t):
                pool.wait_ge(ye_out, t + 1)
                apart(pool)
                pool.dma_start(hidden[t * P:(t + 1) * P, :] if isinstance(t, int) else hidden[bass.ds(t * P, P), :],
                               ye).then_inc(ye_stored, 16)

            with pool.Fori(0, MOE_TILES) as t:
                store_tile(t)
            pool.wait_ge(packed_out, 1)
            pool.wait_ge(ye_stored, 16 * MOE_TILES)
            for s in range(2):
                pick(s, s)
            with pool.Fori(1, TILES // 2) as r:
                for s in range(2):
                    pick(2 * r + s, s)

        @block.vector
        def _(dve):
            dve.wait_ge(setup, 4)
            dve.wait_ge(consts_in, CONSTS)
            nc.vector.tensor_copy(row_next[:], expert_row_sb[:, 1]).then_inc(setup, 1)

            def norm_stats(t, k, src):
                nc.vector.bn_stats(ln[k][:, 0:6], src).then_inc(ln_step[k], 1)
                dve.wait_ge(ln_step[k], t + 1)
                apart(dve)
                nc.vector.bn_aggr(ln[k][:, 6:8], ln[k][:, 0:6]).then_inc(ln_var[k], 1)

            def norm_scale(t, k, src, dst):
                dve.wait_ge(ln_rstd[k], t + 1)
                nc.vector.tensor_scalar(dst, src, ln[k][:, 6:7], ln[k][:, 8:9], ALU.subtract, ALU.mult)\
                    .then_inc(ln_out[k], 1)

            def negative_max(t, u):
                dve.wait_ge(score_done, t * UNITS + u + 1)
                nc.vector.tensor_reduce(neg_max[:, u:u + 1], score_ps[u % 2][:, 0:M], AX, ALU.max, negate=True)\
                    .then_inc(max_done, 1)

            def copy_pt(t, u):
                n = t * UNITS + u
                dve.wait_ge(pt_done, n + 1)
                if not (isinstance(t, int) and n < 2):
                    dve.wait_ge(pv_done, n - 1)
                nc.vector.tensor_copy(prob_t[:, u % 2], pt_ps[:, 0:2 * P].rearrange("p (m n) -> p m n", m=2))\
                    .then_inc(pt_out, 1)

            def fold_o(t, b):
                n = t * BT + b
                dve.wait_ge(pv_done, (n + 1) * G)
                ps = o_ps[:, 0:C * P].rearrange("p (c j n) -> p c j n", c=C, j=JH)
                msk = fold_mask_sb[:].unsqueeze(1).unsqueeze(3).broadcast_to([P, C, JH, NQ])
                nc.vector.tensor_tensor(o_masked[:], ps, msk, ALU.mult).then_inc(o_out, 1)
                dve.wait_ge(o_out, n + 1)
                nc.vector.tensor_reduce(o_t[:, :, b], o_masked[:].rearrange("p c j n -> p c n j"), AX, ALU.add)\
                    .then_inc(o_step, 1)

            norm_src = x_ln1[:]
            dve.wait_ge(xln_in, 16)
            norm_stats(0, 0, norm_src)
            norm_scale(0, 0, norm_src, xn1[:])

            def merge_heads(t):
                dve.wait_ge(av_done, 2 * (t + 1))
                ps = c_ps[:, 0:H * (HD + 1)].rearrange("p (h d) -> p h d", h=H)
                nc.vector.tensor_scalar(den[:], ps[:, :, HD], ATT_EPS, None, ALU.add).then_inc(av_step, 1)
                dve.wait_ge(av_step, t * 2 + 1)
                nc.vector.reciprocal(den[:], den[:]).then_inc(av_step, 1)
                dve.wait_ge(av_step, t * 2 + 2)
                nc.vector.tensor_tensor(merged[:], ps[:, :, 0:HD],
                                        den[:].unsqueeze(2).broadcast_to([P, H, HD]), ALU.mult)\
                    .then_inc(merged_out, 1)

            def finish_cross(t):
                dve.wait_ge(ex_done, t + 1)
                dve.wait_ge(o_step, (t + 1) * BT)
                ex = c_ps[:].rearrange("p (c w n) -> p c w n", c=C, w=2)
                ext = c_ps[:].rearrange("p (c w b n) -> p c w b n", c=C, w=2, b=BT)
                vt = v_tail[:, :, bass.ds(t * BT, BT)].unsqueeze(3).broadcast_to([P, C, BT, NQ])
                nc.vector.tensor_tensor(o_tail[:].rearrange("p c (b n) -> p c b n", b=BT),
                                        ext[:, :, 1], vt, ALU.mult).then_inc(ex_step, 1)
                dve.wait_ge(ex_step, t * 2 + 1)
                nc.vector.tensor_tensor(o_tail[:], o_tail[:], o_t[:].rearrange("p c b n -> p c (b n)"),
                                        ALU.add).then_inc(ex_step, 1)
                dve.wait_ge(ex_step, t * 2 + 2)
                nc.vector.tensor_tensor(o_norm[:], o_tail[:], ex[:, :, 0], ALU.mult).then_inc(norm_out, 1)

            def add_x2(t):
                dve.wait_ge(wo2_done, t + 1)
                dve.wait_ge(x1b_done, t + 1)
                if not first(t):
                    dve.wait_ge(x2_stored, 16 * t)
                nc.vector.tensor_tensor(x2[:], c_ps[:, 0:D], x1[:], ALU.add).then_inc(x2_out, 1)
                dve.wait_ge(x2_out, t + 1)
                norm_stats(t, 2, x2[:])

            def choose(r):
                dve.wait_ge(lg_done, r + 1)
                nc.vector.tensor_copy(logits[:], f_ps[:, 0:E]).then_inc(lg_step, 1)
                dve.wait_ge(lg_step, r * 5 + 1)
                apart(dve)
                nc.vector.max(top[:], logits[:]).then_inc(lg_step, 1)
                dve.wait_ge(lg_step, r * 5 + 2)
                apart(dve)
                nc.vector.max_index(top_at[:], top[:], logits[:]).then_inc(lg_step, 1)
                nc.vector.tensor_copy(tops[:, bass.ds(r, 1)].rearrange("p a k -> p (a k)"), top[:, 0:TOPK])
                dve.wait_ge(lg_step, r * 5 + 3)
                nc.vector.tensor_copy(top_f[:], top_at[:, 0:TOPK]).then_inc(lg_step, 1)
                dve.wait_ge(lg_step, r * 5 + 4)
                nc.vector.tensor_copy(experts[:, bass.ds(r, 1)].rearrange("p a k -> p (a k)"), top_f[:])
                nc.vector.tensor_tensor(chosen[:],
                                        expert_row_sb[:, 0].unsqueeze(1).broadcast_to([P, TOPK, E]),
                                        top_f[:].unsqueeze(2).broadcast_to([P, TOPK, E]), ALU.is_equal)\
                    .then_inc(lg_step, 1)
                dve.wait_ge(lg_step, r * 5 + 5)
                nc.vector.tensor_tensor(chosen_any[:], chosen[:, 0], chosen[:, 1], ALU.add)\
                    .then_inc(any_out, 1)

            def rank(r):
                dve.wait_ge(rank_done, r + 1)
                nc.vector.tensor_tensor(pos[:], f_ps[:, 0:E], row_next[:], ALU.add).then_inc(rank_step, 1)
                dve.wait_ge(rank_step, r * 4 + 1)
                nc.vector.tensor_tensor(row_next[:], f_ps[:, E:2 * E], row_next[:], ALU.add)\
                    .then_inc(rank_step, 1)
                nc.vector.tensor_tensor(pos_chosen[:], chosen[:],
                                        pos[:].unsqueeze(1).broadcast_to([P, TOPK, E]), ALU.mult)\
                    .then_inc(rank_step, 1)
                dve.wait_ge(rank_step, r * 4 + 3)
                nc.vector.tensor_reduce(slot_f[:], pos_chosen[:], AX, ALU.add).then_inc(rank_step, 1)
                dve.wait_ge(rank_step, r * 4 + 4)
                nc.vector.tensor_copy(slots[:, bass.ds(r, 1)].rearrange("p a k -> p (a k)"), slot_f[:])
                if not first(r):
                    dve.wait_ge(routed_out, 32 * r)
                nc.vector.tensor_copy(slot[:], slot_f[:]).then_inc(slot_out, 1)

            def biases(t):
                dve.wait_ge(qk_done, t + 1)
                bqk = bias_qk_sb[:].unsqueeze(2).broadcast_to([P, 4, P])
                nc.vector.tensor_tensor(qk_pre[:], c_ps[:].rearrange("p (k n) -> p k n", k=4), bqk, ALU.add)\
                    .then_inc(qkb_step, 1)
                dve.wait_ge(qkb_step, t + 1)
                nc.vector.tensor_scalar(qk_min[:], qk_pre[:], 0.0, None, ALU.min).then_inc(qkb_out, 1)
                dve.wait_ge(v2_done, t + 1)
                if not first(t):
                    dve.wait_ge(av_done, 2 * t)
                nc.vector.tensor_tensor(v_aug[:, :, 0:HD], f_ps[:, 0:D].rearrange("p (h d) -> p h d", h=H),
                                        bias_sb[:, 1].rearrange("p (h d) -> p h d", h=H), ALU.add)\
                    .then_inc(v2_out, 1)

            def mask_scores(t, g):
                dve.wait_ge(sc2_done, t * G + g + 1)
                src = (c_ps, f_ps)[g % 2][:].rearrange("p (j n) -> p j n", j=JH)
                nc.vector.tensor_tensor(a_t[:, g * JH:(g + 1) * JH], src,
                                        causal_sb[:].unsqueeze(1).broadcast_to([P, JH, P]), ALU.mult)\
                    .then_inc(sc2_out, 1)

            def body(i):
                att, nxt, rest, late = phases(i)
                for u in range(UNITS):
                    if att:
                        negative_max(i, u)
                    if late and u == 0:
                        merge_heads(i - 2)
                    if late and u == 3:
                        add_x2(i - 2)
                    if late and u == 4:
                        if not (isinstance(i, int) and i < 3):
                            dve.wait_ge(routed_out, 32 * (i - 2))
                        norm_scale(i - 2, 2, x2[:], xn3[:])
                    if rest and u == 4:
                        finish_cross(i - 1)
                    if rest and u == 6:
                        dve.wait_ge(wo1_done, i)
                        dve.wait_ge(xb_done, i)
                        nc.vector.tensor_tensor(x1[:], c_ps[:, 0:D], x_res[:], ALU.add).then_inc(x1_out, 1)
                        dve.wait_ge(x1_out, i)
                        norm_stats(i - 1, 1, x1[:])
                    if late and u == 6:
                        choose(i - 2)
                    if rest and u == 7:
                        norm_scale(i - 1, 1, x1[:], xn2[:])
                    if late and u == 8:
                        rank(i - 2)
                    if rest and u == 9:
                        biases(i - 1)
                    if rest and u == 10:
                        dve.wait_ge(qke_out, i)
                        nc.vector.scalar_tensor_tensor(qk_phi[:], qk_pre[:], 0.0, qk_min[:], ALU.max, ALU.add)\
                            .then_inc(phi_out, 1)
                    if rest and u == 12:
                        mask_scores(i - 1, 0)
                        mask_scores(i - 1, 1)
                    if rest and u == 13:
                        mask_scores(i - 1, 2)
                    if rest and u == 14:
                        mask_scores(i - 1, 3)
                    if att and u >= 1:
                        copy_pt(i, u - 1)
                    if rest and u == 0:
                        dve.wait_ge(exp_done, i * UNITS)
                        nc.vector.reciprocal(row_stat[:, :, 0], row_stat[:, :, 0]).then_inc(sums_inverted, 1)
                        copy_pt(i - 1, UNITS - 1)
                    if att and u >= 2 and (u - 2) % G == 3:
                        fold_o(i, (u - 2) // G)
                    if rest and u == 1:
                        fold_o(i - 1, BT - 1)
                    if nxt and u == 2:
                        dve.wait_ge(xln_in, 16 * (i + 2))
                        norm_stats(i + 1, 0, x_ln1[:])
                    if nxt and u == 5:
                        dve.wait_ge(xt_done[0], i + 1)
                        norm_scale(i + 1, 0, x_ln1[:], xn1[:])
            iterations(dve, body)

            n_steps = [0]

            def step(ins):
                n_steps[0] += 1
                ins.then_inc(plan_step, 1)
                dve.wait_ge(plan_step, n_steps[0])

            count, n_tiles, end, skip = (plan[:, k, 0:E] for k in range(4))
            expert_of, row_of, passed, jump = (plan[:, k] for k in range(4, 8))
            base = expert_row_sb[:, 1]
            taken = plan_i[:, 2, 0:E]
            dve.wait_ge(rank_step, 4 * TILES)
            step(nc.vector.tensor_copy(taken, row_next[:]))
            step(nc.vector.tensor_tensor(count, row_next[:], base, ALU.subtract))
            step(nc.vector.tensor_scalar(count, count, float(P - 1), None, ALU.add))
            tiles_i = plan_i[:, 0, 0:E]
            step(nc.vector.tensor_copy(tiles_i, count))
            step(nc.vector.tensor_scalar(tiles_i, tiles_i, 7, None, ALU.logical_shift_right))
            step(nc.vector.tensor_copy(n_tiles, tiles_i))
            step(nc.vector.tensor_copy(end[:, 0:1], n_tiles[:, 0:1]))
            for e in range(1, E):
                step(nc.vector.tensor_tensor(end[:, e:e + 1], end[:, e - 1:e], n_tiles[:, e:e + 1], ALU.add))
            step(nc.vector.tensor_scalar(skip, n_tiles, float(-P), float(REGION), ALU.mult, ALU.add))
            step(nc.vector.memset(expert_of, 0.0))
            step(nc.vector.tensor_scalar(row_of, tile_row_sb[:], float(P), None, ALU.mult))
            for e in range(E - 1):
                step(nc.vector.tensor_scalar(passed, tile_row_sb[:], end[:, e:e + 1], None, ALU.is_ge))
                step(nc.vector.tensor_tensor(expert_of, expert_of, passed, ALU.add))
                step(nc.vector.scalar_tensor_tensor(row_of, passed, skip[:, e:e + 1], row_of, ALU.mult, ALU.add))
            last = jump[:, 0:1]
            step(nc.vector.tensor_scalar(last, n_tiles[:, E - 1:E], -1.0, 0.0, ALU.add, ALU.max))
            step(nc.vector.tensor_scalar(last, last, float(P), float((E - 1) * REGION), ALU.mult, ALU.add))
            step(nc.vector.tensor_scalar(row_of, row_of, last, None, ALU.min))
            step(nc.vector.tensor_copy(plan_i[:, 0], expert_of))
            nc.vector.tensor_copy(plan_i[:, 1], row_of).then_inc(plan_out, 1)

            step(nc.vector.tensor_scalar(skip, skip, -1.0, None, ALU.mult))
            for e in range(E - 1):
                step(nc.vector.tensor_scalar(behind[:], experts[:], float(e), None, ALU.is_gt))
                step(nc.vector.scalar_tensor_tensor(slots[:], behind[:], skip[:, e:e + 1], slots[:],
                                                    ALU.mult, ALU.add))
            nc.vector.tensor_copy(packed[:], slots[:]).then_inc(packed_out, 1)

            tv = tops[:].rearrange("p t k -> p k t")
            nc.vector.tensor_tensor(weight[:, 1], tv[:, 1], tv[:, 0], ALU.subtract).then_inc(weight_exp, 1)
            dve.wait_ge(weight_exp, 2)
            nc.vector.tensor_scalar(weight[:, 0], weight[:, 1], 1.0, None, ALU.add).then_inc(weight_out, 1)
            dve.wait_ge(weight_out, 1)
            nc.vector.reciprocal(weight[:, 0], weight[:, 0]).then_inc(weight_out, 1)
            dve.wait_ge(weight_out, 2)
            nc.vector.tensor_tensor(weight[:, 1], weight[:, 1], weight[:, 0], ALU.mult).then_inc(weight_out, 1)

            def copy_xe(t):
                dve.wait_ge(xet_done, t + 1)
                nc.vector.tensor_copy(xe_t[:], bank[2][:, 0:C * P].rearrange("p (c n) -> p c n", c=C))\
                    .then_inc(xet_out, 1)

            def hidden_rows(t):
                dve.wait_ge(sig_out, t + 1)
                nc.vector.tensor_tensor(gate, bank[0][:], gate, ALU.mult).then_inc(hid_step, 1)
                dve.wait_ge(hid_step, t + 1)
                dve.wait_ge(gv_done, t + 1)
                if not first(t):
                    dve.wait_ge(ht_done, t)
                nc.vector.tensor_tensor(hid, bank[1][:], gate, ALU.mult).then_inc(hid_out, 1)

            def copy_y(t):
                dve.wait_ge(y_done, t + 1)
                if not first(t):
                    dve.wait_ge(ye_stored, 16 * t)
                nc.vector.tensor_copy(ye, bank[4][:, 0:D]).then_inc(ye_out, 1)

            copy_xe(0)
            hidden_rows(0)
            copy_xe(1)
            with dve.Fori(1, MOE_TILES - 1) as t:
                hidden_rows(t)
                copy_xe(t + 1)
                copy_y(t - 1)
            hidden_rows(MOE_TILES - 1)
            copy_y(MOE_TILES - 2)
            copy_y(MOE_TILES - 1)

            def combine(t, r, s):
                dve.wait_ge(picked[s], 32 * (r + 1))
                dve.wait_ge(back_in[s], 16 * (r + 1))
                if not first(r):
                    dve.wait_ge(stored[s], 16 * r)
                nc.vector.scalar_tensor_tensor(y_out[:, s], y_pick[:, s, 0], weight[:, 0, bass.ds(t, 1)],
                                               x2_back[:, s], ALU.mult, ALU.add).then_inc(sum_step, 1)
                dve.wait_ge(sum_step, t + 1)
                nc.vector.scalar_tensor_tensor(y_out[:, s], y_pick[:, s, 1], weight[:, 1, bass.ds(t, 1)],
                                               y_out[:, s], ALU.mult, ALU.add).then_inc(sum_out, 1)

            dve.wait_ge(weight_out, 3)
            for s in range(2):
                combine(s, 0, s)
            with dve.Fori(1, TILES // 2) as r:
                for s in range(2):
                    combine(2 * r + s, r, s)

        @block.tensor
        def _(pe):
            mm, tr = nc.tensor.matmul, nc.tensor.transpose
            pe.wait_ge(consts_in, CONSTS)

            def transposed(dst, src, sem_):
                for c in range(C):
                    last = tr(dst[:, c * P:(c + 1) * P], src[:, c * P:(c + 1) * P], ident_sb[:])
                last.then_inc(sem_, 1)

            def project(t, b, k):
                n = (t * BT + b) * 3 + k
                if k == 0:
                    pe.wait_ge(ctx_in[b], 16 * (t + 1))
                if not (isinstance(t, int) and n < 2):
                    pe.wait_ge(proj_out, n - 1)
                dst = proj_ps[(b * 3 + k) % 2]
                if k < 2:
                    for d in range(C):
                        last = mm(dst[:, 0:M], w_sb[:, WK1, d, k * P:(k + 1) * P], ctx_sb[:, b, d],
                                  start=(d == 0), stop=(d == C - 1))
                else:
                    for m in range(2):
                        for d in range(C):
                            last = mm(dst[:, m * D:(m + 1) * D], ctx_sb[:, b, d, m * P:(m + 1) * P],
                                      w_sb[:, WV1, d], start=(d == 0), stop=(d == C - 1))
                last.then_inc(proj_done, 1)

            def scores(t, u):
                b, g = u // G, u % G
                n = t * UNITS + u
                if g == 0:
                    pe.wait_ge(heads_done, t * BT + b + 1)
                    pe.wait_ge(proj_out, (t * BT + b) * 3 + 2)
                if not (isinstance(t, int) and n < 2):
                    pe.wait_ge(exp_done, n - 1)
                c, half = g // 2, g % 2
                q = q_heads[:, b % 2, c, half * JH:(half + 1) * JH].rearrange("p j n -> p (j n)")
                mm(score_ps[u % 2][:, 0:M], q, k_t[:, b % 2, c], start=True, stop=True).then_inc(score_done, 1)

            def transpose_probs(t, u):
                n = t * UNITS + u
                pe.wait_ge(exp_done, n + 1)
                if not (isinstance(t, int) and n < 1):
                    pe.wait_ge(pt_out, n)
                for m in range(2):
                    last = tr(pt_ps[:, m * P:(m + 1) * P], prob[:, u % P_SLOTS, m * P:(m + 1) * P], ident_sb[:])
                last.then_inc(pt_done, 1)

            def values(t, u):
                b, g = u // G, u % G
                n = t * UNITS + u
                pe.wait_ge(pt_out, n + 1)
                if g == 0:
                    pe.wait_ge(proj_out, (t * BT + b) * 3 + 3)
                    if not (isinstance(t, int) and t * BT + b < 1):
                        pe.wait_ge(o_out, t * BT + b)
                c, half = g // 2, g % 2
                for m in range(2):
                    last = mm(o_ps[64 * half:64 * half + 64, c * P:(c + 1) * P],
                              v_sb[:, b % 2, m, g * 64:(g + 1) * 64], prob_t[:, u % 2, m],
                              start=(m == 0), stop=(m == 1))
                last.then_inc(pv_done, 1)

            def query(t):
                pe.wait_ge(xt_out[0], t + 1)
                for c in range(C):
                    for d in range(C):
                        last = mm(f_ps[:, c * P:(c + 1) * P], w_sb[:, WQ1, d, c * P:(c + 1) * P], xn1_t[:, d],
                                  start=(d == 0), stop=(d == C - 1))
                last.then_inc(q_done, 1)

            for c in range(C):
                for d in range(C):
                    last = mm(f_ps[:, c * B:(c + 1) * B], w_sb[:, WV1, d, c * P:(c + 1) * P], tail_sb[:, d],
                              start=(d == 0), stop=(d == C - 1))
            last.then_inc(tail_done, 1)
            pe.wait_ge(tail_out, 1)
            pe.wait_ge(ln_out[0], 1)
            transposed(f_ps, xn1, xt_done[0])
            query(0)
            for k in range(3):
                project(0, 0, k)

            def body(i):
                att, nxt, rest, late = phases(i)
                t, r = i - 1, i - 2
                for u in range(UNITS):
                    b, g = u // G, u % G
                    if att:
                        scores(i, u)
                        if g < 3 and b < 3:
                            project(i, b + 1, g)
                        elif g < 3 and nxt:
                            project(i + 1, 0, g)
                    if att and u >= 2:
                        values(i, u - 2)
                    if rest and u < 2:
                        values(t, UNITS - 2 + u)
                    if att and u >= 1:
                        transpose_probs(i, u - 1)
                    if rest and u == 0:
                        transpose_probs(t, UNITS - 1)
                    if late and u == 1:
                        pe.wait_ge(merged_out, r + 1)
                        transposed(c_ps, merged[:].rearrange("p h d -> p (h d)"), mt_done)
                    if late and u == 2:
                        pe.wait_ge(mt_out, r + 1)
                        for c in range(C):
                            last = mm(c_ps[:, 0:D], merged_t[:, c], w_sb[:, WO2, c], start=(c == 0), stop=(c == C - 1))
                        last.then_inc(wo2_done, 1)
                    if rest and u == 3:
                        pe.wait_ge(stats_done, t + 1)
                        if late:
                            pe.wait_ge(x2_out, r + 1)
                        for c in range(C):
                            for half in range(2):
                                last = mm(c_ps[:, c * 2 * P:(c + 1) * 2 * P], expand_sb[:, half],
                                          stat_rows[:, 2 * c + half].rearrange("p w n -> p (w n)"),
                                          start=(half == 0), stop=(half == 1))
                        last.then_inc(ex_done, 1)
                    if late and u == 4:
                        pe.wait_ge(ln_out[2], r + 1)
                        transposed(f_ps, xn3, xt_done[2])
                    if late and u == 5:
                        pe.wait_ge(xt_out[2], r + 1)
                        for d in range(C):
                            last = mm(f_ps[:, 0:E], xn3_t[:, d], wg_sb[:, d], start=(d == 0), stop=(d == C - 1))
                        last.then_inc(lg_done, 1)
                    if rest and u == 5:
                        pe.wait_ge(norm_out, t + 1)
                        for c in range(C):
                            last = mm(c_ps[:, 0:D], o_norm[:, c], w_sb[:, WO1, c], start=(c == 0), stop=(c == C - 1))
                        last.then_inc(wo1_done, 1)
                    if late and u == 7:
                        pe.wait_ge(any_out, r + 1)
                        for k in range(2):
                            last = mm(f_ps[:, k * E:(k + 1) * E], tri_sb[:, k], chosen_any[:], start=True, stop=True)
                        last.then_inc(rank_done, 1)
                    if rest and u == 7:
                        pe.wait_ge(ln_out[1], t + 1)
                        transposed(c_ps, xn2, xt_done[1])
                    if rest and u == 8:
                        pe.wait_ge(xt_out[1], t + 1)
                        for k in range(4):
                            w, c = (WQ2, WK2)[k // C], k % C
                            for d in range(C):
                                last = mm(c_ps[:, k * P:(k + 1) * P], w_sb[:, w, d, c * P:(c + 1) * P], xn2_t[:, d],
                                          start=(d == 0), stop=(d == C - 1))
                        last.then_inc(qk_done, 1)
                        if late:
                            pe.wait_ge(rank_step, 4 * r + 3)
                        for d in range(C):
                            last = mm(f_ps[:, 0:D], xn2_t[:, d], w_sb[:, WV2, d], start=(d == 0), stop=(d == C - 1))
                        last.then_inc(v2_done, 1)
                    if nxt and u == 9:
                        pe.wait_ge(ln_out[0], i + 2)
                        if rest:
                            pe.wait_ge(v2_out, t + 1)
                        transposed(f_ps, xn1, xt_done[0])
                    if rest and u in (11, 12, 13):
                        for g2 in ((0, 1), (2,), (3,))[u - 11]:
                            if g2 % 2 == 0:
                                pe.wait_ge(phiq_out, t * C + g2 // 2 + 1)
                                pe.wait_ge(v2_out, t + 1)
                            if g2 >= 2:
                                pe.wait_ge(sc2_out, t * G + g2 - 1)
                            if g2 == 1 and nxt:
                                pe.wait_ge(xt_out[0], i + 2)
                            if g2 == 3 and nxt:
                                pe.wait_ge(q_out, i + 2)
                            c, half = g2 // 2, g2 % 2
                            mm((c_ps, f_ps)[g2 % 2][:], qk_phi[:, C + c],
                               phi_heads[:, c, half * JH:(half + 1) * JH].rearrange("p j n -> p (j n)"),
                               start=True, stop=True).then_inc(sc2_done, 1)
                    if nxt and u == 12:
                        if rest:
                            pe.wait_ge(sc2_out, t * G + 2)
                        query(i + 1)
                    if rest and u in (14, 15):
                        pe.wait_ge(sc2_out, t * G + (3, 4)[u - 14])
                        for h in range((u - 14) * H // 2, (u - 13) * H // 2):
                            last = mm(c_ps[:, h * (HD + 1):(h + 1) * (HD + 1)], a_t[:, h], v_aug[:, h],
                                      start=True, stop=True)
                        last.then_inc(av_done, 1)
            iterations(pe, body)

            pe.wait_ge(experts_in, EXPERTS)
            pe.wait_ge(plan_out, 1)

            def transpose_x(t):
                pe.wait_ge(xe_in, 16 * (t + 1))
                transposed(bank[2], xe, xet_done)

            def up_part(t, k):
                w, dst, done, read = ((w1_sb, bank[0], u_done, hid_step), (w2_sb, bank[1], gv_done, hid_out))[k]
                e = pe.value_load(plan_i[0:1, 0, bass.ds(t, 1)], min_val=0, max_val=E - 1)
                pe.wait_ge(xet_out, t + 1)
                if not first(t):
                    pe.wait_ge(read, t)
                for d in range(C):
                    last = mm(dst[:], xe_t[:, d], w[:, bass.ds(e, 1), d].rearrange("p a f -> p (a f)"),
                              start=(d == 0), stop=(d == C - 1))
                last.then_inc(done, 1)

            def transpose_h(t):
                pe.wait_ge(hid_out, t + 1)
                for c in range(FC):
                    last = tr(bank[3][:, c * P:(c + 1) * P], hid[:, c * P:(c + 1) * P], ident_sb[:])
                last.then_inc(ht_done, 1)

            def down(t):
                e = pe.value_load(plan_i[0:1, 0, bass.ds(t, 1)], min_val=0, max_val=E - 1)
                pe.wait_ge(ht_out, t + 1)
                if not first(t):
                    pe.wait_ge(ye_out, t)
                for c in range(FC):
                    last = mm(bank[4][:, 0:D], hid_t[:, c], w3_sb[:, bass.ds(e, 1), c].rearrange("p a d -> p (a d)"),
                              start=(c == 0), stop=(c == FC - 1))
                last.then_inc(y_done, 1)

            transpose_x(0)
            up_part(0, 0)
            up_part(0, 1)
            transpose_x(1)
            with pe.Fori(1, MOE_TILES - 1) as t:
                up_part(t, 0)
                transpose_h(t - 1)
                up_part(t, 1)
                transpose_x(t + 1)
                down(t - 1)
            up_part(MOE_TILES - 1, 0)
            transpose_h(MOE_TILES - 2)
            up_part(MOE_TILES - 1, 1)
            down(MOE_TILES - 2)
            transpose_h(MOE_TILES - 1)
            down(MOE_TILES - 1)


def kernel(x, ctx_1024, L0_xattn_wq, L0_xattn_wk, L0_xattn_wv, L0_xattn_wo, L0_xattn_bo, L0_attn_mask,
           L0_attn_Wq, L0_attn_bq, L0_attn_Wk, L0_attn_bk, L0_attn_Wv, L0_attn_bv, L0_attn_Wo, L0_attn_bo,
           L0_ffn_Wg, L0_ffn_W1, L0_ffn_W2, L0_ffn_W3):
    import numpy as np
    import concourse.bacc as bacc
    from concourse.bass_utils import run_bass_kernel_spmd as run

    def lay(a):
        return np.ascontiguousarray(a)

    ctx = np.asarray(ctx_1024)
    rows = np.arange(P)
    head_of = (rows % 64) // HD
    half_of = rows // 64
    arrays = {
        "x": lay(np.asarray(x).reshape(TILES, P, D)),
        "ctx_t": lay(ctx.reshape(TILES, BT, M, C, P).transpose(0, 1, 4, 3, 2)),
        "tail_t": lay(ctx[:, M - 1].reshape(B, C, P).transpose(2, 1, 0)),
        "w_attn": lay(np.stack([np.asarray(w).T.reshape(C, P, D).transpose(1, 0, 2) for w in (
            L0_xattn_wq, L0_xattn_wk, L0_xattn_wv, L0_xattn_wo,
            L0_attn_Wq, L0_attn_Wk, L0_attn_Wv, L0_attn_Wo)], axis=1)),
        "bias_rows": lay(np.stack([np.asarray(v) for v in (L0_xattn_bo, L0_attn_bv, L0_attn_bo)])),
        "bias_qk": lay(np.stack([np.asarray(L0_attn_bq).reshape(C, P), np.asarray(L0_attn_bk).reshape(C, P)])
                       .reshape(2 * C, P).T),
        "wg": lay(np.asarray(L0_ffn_Wg).reshape(C, P, E).transpose(1, 0, 2)),
        "w_expert": lay(np.concatenate([np.asarray(w).reshape(E, n, P, -1).transpose(0, 2, 1, 3).reshape(E, P, C * F)
                                        for w, n in ((L0_ffn_W1, C), (L0_ffn_W2, C), (L0_ffn_W3, FC))])),
        "ident": np.eye(P, dtype=np.float32),
        "head_mask": lay((half_of[:, None] * JH + head_of[:, None] == np.arange(2 * JH)[None]).astype(np.float32)),
        "fold_mask": lay((head_of[:, None] == np.arange(JH)[None]).astype(np.float32)),
        "causal": lay(((rows[:, None] // NQ == rows[None] // NQ) & (rows[:, None] <= rows[None])).astype(np.float32)),
        "tri": lay(np.stack([rows[:, None] < rows[None], rows[:, None] >= 0 * rows[None]], axis=1).astype(np.float32)),
        "expand": lay(np.stack([(half_of[None] == half) & (rows[:, None] // NQ == head_of[None])
                                for half in range(2)], axis=1).astype(np.float32)),
        "query_eye": lay((rows[:, None] % NQ == np.arange(NQ)[None]).astype(np.float32)),
        "expert_row": lay(np.broadcast_to(np.stack([np.arange(E), np.arange(E) * REGION])[None],
                                          (P, 2, E)).astype(np.float32)),
        "tile_row": lay(np.broadcast_to(np.arange(MOE_TILES, dtype=np.float32)[None], (P, MOE_TILES))),
    }
    nc = bacc.Bacc("TRN2", target_bir_lowering=False, num_devices=1)
    aps = {k: nc.dram_tensor(k, v.shape, mybir.dt.from_np(v.dtype), kind="ExternalInput").ap()
           for k, v in arrays.items()}
    f32 = mybir.dt.float32
    routed = nc.dram_tensor("routed", (E * REGION, D), f32, kind="Internal").ap()
    hidden = nc.dram_tensor("hidden", (MOE_TILES * P, D), f32, kind="Internal").ap()
    x2_dram = nc.dram_tensor("x2_dram", (TILES, P, D), f32, kind="Internal").ap()
    out = nc.dram_tensor("out", (TILES, P, D), f32, kind="ExternalOutput").ap()
    perceiver(nc, **aps, routed=routed, hidden=hidden, x2_dram=x2_dram, out=out)
    got = run(nc, [arrays], core_ids=[0])
    return got.results[0]["out"].reshape(B, NQ, D)
```

```python
from contextlib import ExitStack

import concourse.bass as bass
from concourse import mybir

B, NQ, D = 128, 32, 256
M = 257
H, HD = 16, 16
E, F = 8, 512
P = 128
TOK = B * NQ
TILES = TOK // P
BT = P // NQ
C = D // P
G = 4
JH = H // G
UNITS = BT * G
FC = F // P
REGION = TOK + P
TOPK = 2
MOE_TILES = TOPK * TOK // P + E - 1
LN_EPS = 1e-5
ATT_EPS = 1e-6
WQ1, WO1, WQ2, WK2, WV2, WO2 = range(6)
M_EVEN = M + 1
HI, LO = 0, 1
PASSES = ((HI, HI), (HI, LO), (LO, HI))
ROW = D + 2
SPARE = E * REGION
W_EXPERT = 3 * C * F
PIECE = E * W_EXPERT // TILES
W_PARTS = W_EXPERT // PIECE
EARLY, MIDDLE = 3, 6
P_SLOTS = 4


def first(t):
    return isinstance(t, int) and t == 0


def perceiver(nc, x, ctx_t, tail_t, w_attn, w_kv, bias_rows, bias_qk, wg, w_expert,
              ident, head_mask, fold_mask, causal, tri, expand, query_eye, expert_row, tile_row, token_row,
              routed, w_rest, out):
    f32 = mybir.dt.float32
    f32r = mybir.dt.float32r
    i32 = mybir.dt.int32
    u32 = mybir.dt.uint32
    ACT = mybir.ActivationFunctionType
    ALU = mybir.AluOpType
    AX = mybir.AxisListType.X

    with ExitStack() as stack:
        def sb(name, shape, dt=f32):
            return stack.enter_context(nc.sbuf_tensor(name, shape, dt))

        def sem(name):
            return stack.enter_context(nc.semaphore(name))

        def att(name, shape, dt=f32):
            return attention.enter_context(nc.sbuf_tensor(name, shape, dt))

        ident_sb = sb("ident_sb", [P, P])
        expert_row_sb = sb("expert_row_sb", [P, 2, E])
        tile_row_sb = sb("tile_row_sb", [P, MOE_TILES])
        neg_half = sb("neg_half", [P, 1])
        row_next = sb("row_next", [P, E])
        plan_i = sb("plan_i", [P, 3, MOE_TILES], i32)
        padding = sb("padding", [P, ROW])
        to_row = sb("to_row", [P, 1], i32)
        expert_hi = sb("expert_hi", [P, E * W_EXPERT], f32r)

        attention = ExitStack()
        kv_hi = att("kv_hi", [P, 2, C, D], f32r)
        kv_lo = att("kv_lo", [P, 2, C, D], f32r)
        ctx_sb = att("ctx_sb", [P, C, M_EVEN])
        ctx_hi = att("ctx_hi", [P, 2, C, M_EVEN], f32r)
        ctx_lo = att("ctx_lo", [P, 2, C, M_EVEN], f32r)
        k_hi = att("k_hi", [P, 2, C, M_EVEN], f32r)
        k_lo = att("k_lo", [P, 2, C, M_EVEN], f32r)
        v_sb = att("v_sb", [P, 2, 2, D])
        x_ln1 = att("x_ln1", [P, D])
        xn1 = att("xn1", [P, D])
        xn1_t = att("xn1_t", [P, C, P])
        q_t = att("q_t", [P, C, P])
        q_hi = att("q_hi", [P, C, P], f32r)
        q_lo = att("q_lo", [P, C, P], f32r)
        heads_hi = att("heads_hi", [P, 2, C, 2 * JH, NQ], f32r)
        heads_lo = att("heads_lo", [P, 2, C, 2 * JH, NQ], f32r)
        prob = att("prob", [P, P_SLOTS, M])
        prob_t = att("prob_t", [P, 2, 2, P])
        o_masked = att("o_masked", [P, C, JH, NQ])

        head_mask_sb = att("head_mask_sb", [P, 2 * JH])
        scaled_mask_sb = att("scaled_mask_sb", [P, 2 * JH])
        fold_mask_sb = att("fold_mask_sb", [P, JH])
        causal_sb = att("causal_sb", [P, P])
        expand_sb = att("expand_sb", [P, 64])
        query_eye_sb = att("query_eye_sb", [P, NQ])
        bias_qk_sb = att("bias_qk_sb", [P, 4])
        v_tail = att("v_tail", [P, C, B])
        neg_max = att("neg_max", [P, UNITS])
        row_sum = att("row_sum", [P, G, BT])
        inv_stat = att("inv_stat", [P, G, 2, BT])
        o_t = att("o_t", [P, C, BT, NQ])
        stat_rows = att("stat_rows", [P, G, 2 * BT, NQ])
        o_tail = att("o_tail", [P, C, P])
        x_res = att("x_res", [P, D])
        xn2 = att("xn2", [P, D])
        xn2_t = att("xn2_t", [P, C, P])
        qk_phi = att("qk_phi", [P, 4, P])
        qk_min = att("qk_min", [P, 4, P])
        phi_heads = att("phi_heads", [P, C, 2 * JH, P])
        a_t = att("a_t", [P, H, P])
        bias_sb = att("bias_sb", [P, 3, D])
        v_aug = att("v_aug", [P, H, HD + 1])
        token_row_sb = att("token_row_sb", [P, 2])
        w_sb = att("w_sb", [P, 6, C, D])

        merged = att("merged", [P, H, HD])
        merged_t = att("merged_t", [P, C, P])
        x1 = att("x1", [P, D])
        x2 = att("x2", [P, D])
        xn3 = att("xn3", [P, TOPK, ROW])
        xn3_t = att("xn3_t", [P, C, P])
        den = att("den", [P, H])
        ln = [att(f"ln{k}", [P, 16]) for k in range(3)]
        logits = att("logits", [P, E])
        top = att("top", [P, E])
        top_at = att("top_at", [P, E], u32)
        top_f = att("top_f", [P, TOPK])
        chosen = att("chosen", [P, TOPK, E])
        chosen_any = att("chosen_any", [P, E])
        pos = att("pos", [P, E])
        pos_chosen = att("pos_chosen", [P, TOPK, E])
        slot_f = att("slot_f", [P, TOPK])
        slot = att("slot", [P, TOPK], i32)
        exp_gap = att("exp_gap", [P, 2])
        pair_weight = att("pair_weight", [P, TOPK])
        token_no = att("token_no", [P, 1])
        wg_sb = att("wg_sb", [P, C, E])
        tri_sb = att("tri_sb", [P, 2, P])
        attention.close()

        spare = a_t[:].rearrange("p h n -> p (h n)")
        kv_raw = spare[:, 0:2 * C * D].rearrange("p (k c d) -> p k c d", k=2, c=C)
        tail_sb = spare[:, 2 * C * D:2 * C * D + C * B].rearrange("p (c b) -> p c b", c=C)
        piece = phi_heads[:].rearrange("p c j n -> p (c j n)")[:, 0:PIECE]

        plan = sb("plan", [P, 7, MOE_TILES])
        row_info = sb("row_info", [P, MOE_TILES, 2])
        xe = sb("xe", [P, ROW])
        xe_hi = sb("xe_hi", [P, C, P], f32r)
        xe_lo = sb("xe_lo", [P, C, P], f32r)
        hid = sb("hid", [P, F])
        hid_hi = sb("hid_hi", [P, FC, P], f32r)
        hid_lo = sb("hid_lo", [P, FC, P], f32r)
        ye = sb("ye", [P, D])
        expert_lo = sb("expert_lo", [P, E * W_EXPERT], f32r)

        def expert_weights(w, e):
            cols = slice(w * C * F, (w + 1) * C * F)
            return [x[:].rearrange("p (e n) -> p e n", e=E)[:, bass.ds(e, 1), cols]
                    .rearrange("p a (k n) -> p (a k) n", k=C if w < 2 else FC) for x in (expert_hi, expert_lo)]

        bank = [stack.enter_context(nc.psum_tensor(f"bank{k}", [P, 512], f32)) for k in range(8)]
        proj_ps = bank[0:2]
        score_ps = bank[2:4]
        pt_ps, o_ps, c_ps, f_ps = bank[4:8]

        first_in, consts_in, later_in = sem("first_in"), sem("consts_in"), sem("later_in")
        kv_hi_out, kv_lo_out = sem("kv_hi_out"), sem("kv_lo_out")
        ctx_hi_out, ctx_lo_out = sem("ctx_hi_out"), sem("ctx_lo_out")
        piece_in, piece_hi_out, piece_lo_out, piece_stored, rest_in = (
            sem("piece_in"), sem("piece_hi_out"), sem("piece_lo_out"), sem("piece_stored"), sem("rest_in"))
        tail_done, tail_out = sem("tail_done"), sem("tail_out")
        ctx_in = sem("ctx_in")
        xln_in, xres_in = sem("xln_in"), sem("xres_in")
        proj_done, proj_out = sem("proj_done"), sem("proj_out")
        score_done, max_done, exp_done = sem("score_done"), sem("max_done"), sem("exp_done")
        pt_done, pt_out, pv_done, o_out = sem("pt_done"), sem("pt_out"), sem("pv_done"), sem("o_out")
        o_step = sem("o_step")
        heads_done = sem("heads_done")
        sums_inverted = sem("sums_inverted")
        last_copied, stats_done = sem("last_copied"), sem("stats_done")
        ln_step = [sem(f"ln_step{k}") for k in range(3)]
        ln_var = [sem(f"ln_var{k}") for k in range(3)]
        ln_eps_done = [sem(f"ln_eps_done{k}") for k in range(3)]
        ln_rstd = [sem(f"ln_rstd{k}") for k in range(3)]
        ln_out = [sem(f"ln_out{k}") for k in range(3)]
        xt_done = [sem(f"xt_done{k}") for k in range(3)]
        xt_out = [sem(f"xt_out{k}") for k in range(3)]
        k_lo_out = sem("k_lo_out")
        q_done, q_out, q_lo_out = sem("q_done"), sem("q_out"), sem("q_lo_out")
        ex_done, ex_step, norm_out = sem("ex_done"), sem("ex_step"), sem("norm_out")
        wo1_done, xb_done, x1_out, x1b_done = sem("wo1_done"), sem("xb_done"), sem("x1_out"), sem("x1b_done")
        qk_done, v2_done, v2_out = sem("qk_done"), sem("v2_done"), sem("v2_out")
        qkb_step, qkb_out, qke_out, phi_out, phi0_out, phi1_out = (sem("qkb_step"), sem("qkb_out"), sem("qke_out"),
                                                         sem("phi_out"), sem("phi0_out"), sem("phi1_out"))
        sc2_done, sc2_out = sem("sc2_done"), sem("sc2_out")
        av_done, av_step, merged_out = sem("av_done"), sem("av_step"), sem("merged_out")
        mt_done, mt_out = sem("mt_done"), sem("mt_out")
        wo2_done, x2_out, x2_stored = sem("wo2_done"), sem("x2_out"), sem("x2_stored")
        lg_done, lg_step, any_out, rank_done, rank_step, slot_out = (
            sem("lg_done"), sem("lg_step"), sem("any_out"), sem("rank_done"), sem("rank_step"), sem("slot_out"))
        routed_out = sem("routed_out")
        setup = sem("setup")
        plan_step, taken_out, plan_out, zero_in = (sem("plan_step"), sem("taken_out"), sem("plan_out"),
                                                   sem("zero_in"))
        gap_out, gap_exp, weight_step, pair_out, rows_ready = (
            sem("gap_out"), sem("gap_exp"), sem("weight_step"), sem("pair_out"), sem("rows_ready"))
        twin_out, info_kept, to_row_out = sem("twin_out"), sem("info_kept"), sem("to_row_out")
        xe_in, xet_done, xe_hi_out, xe_lo_out = sem("xe_in"), sem("xet_done"), sem("xe_hi_out"), sem("xe_lo_out")
        u_done, gv_done, sig_out, hid_step, hid_out = (sem("u_done"), sem("gv_done"), sem("sig_out"),
                                                       sem("hid_step"), sem("hid_out"))
        hid_lo_out = sem("hid_lo_out")
        ht_done, ht_out, y_done, ye_out, ye_stored = (sem("ht_done"), sem("ht_out"), sem("y_done"),
                                                      sem("ye_out"), sem("ye_stored"))
        waits_passed = sem("waits_passed")
        FIRST = 16 * 4
        CONSTS = 16 * 12

        block = stack.enter_context(nc.Block())

        def phases(i):
            if not isinstance(i, int):
                return True, True, True, True
            return i < TILES, i + 1 < TILES, 1 <= i <= TILES, 2 <= i <= TILES + 1

        def apart(engine):
            engine.sem_inc(waits_passed, 1)

        def split_phi(engine, c):
            src = qk_phi[:, c].unsqueeze(1).broadcast_to([P, 2 * JH, P])
            msk = head_mask_sb[:].unsqueeze(2).broadcast_to([P, 2 * JH, P])
            return engine.tensor_tensor(phi_heads[:, c], src, msk, ALU.mult)

        def iterations(engine, body):
            for i in range(3):
                body(i)
            with engine.Fori(3, TILES - 1) as i:
                body(i)
            for i in range(TILES - 1, TILES + 2):
                body(i)

        @block.sync
        def _(sp):
            def load_ctx(t, b):
                n = t * BT + b
                if not (isinstance(t, int) and n < 1):
                    sp.wait_ge(ctx_lo_out, n)
                sp.dma_start(ctx_sb[:, :, 0:M], ctx_t[t, b]).then_inc(ctx_in, 16)

            def load_xln(t):
                if not first(t):
                    sp.wait_ge(ln_out[0], t)
                sp.dma_start(x_ln1[:], x[t]).then_inc(xln_in, 16)

            def load_xres(t):
                if not first(t):
                    sp.wait_ge(x1_out, t)
                sp.dma_start(x_res[:], x[t]).then_inc(xres_in, 16)

            load_xln(0)
            sp.dma_start(kv_raw, w_kv).then_inc(first_in, 16)
            load_ctx(0, 0)
            sp.dma_start(w_sb[:, WQ1], w_attn[:, WQ1]).then_inc(first_in, 16)
            sp.dma_start(tail_sb, tail_t).then_inc(consts_in, 16)
            sp.dma_start(bias_sb[:].rearrange("p k d -> p (k d)"), bias_rows.broadcast_to([P, 3 * D]))\
                .then_inc(consts_in, 16)
            sp.dma_start(w_sb[:, WO1:], w_attn[:, WO1:]).then_inc(later_in, 16)
            load_ctx(0, 1)
            load_xres(0)

            def body(i):
                att, nxt, rest, late = phases(i)
                if nxt:
                    load_xln(i + 1)
                if att:
                    load_ctx(i, 2)
                    if not first(i):
                        sp.wait_ge(piece_stored, 16 * i)
                    if not (isinstance(i, int) and i < 2):
                        sp.wait_ge(sc2_done, (i - 1) * G)
                    sp.dma_start(piece, w_expert[i]).then_inc(piece_in, 16)
                    load_ctx(i, 3)
                if late:
                    sp.wait_ge(x2_out, i - 1)
                    sp.dma_start(out[i - 2], x2[:]).then_inc(x2_stored, 16)
                if nxt:
                    load_ctx(i + 1, 0)
                if rest and att:
                    load_xres(i)
                if att:
                    sp.wait_ge(piece_lo_out, i + 1)
                    sp.dma_start(w_rest[i], piece).then_inc(piece_stored, 16)
                if nxt:
                    load_ctx(i + 1, 1)

            iterations(sp, body)

            sp.dma_start(routed[SPARE:SPARE + P, :], padding[:]).then_inc(zero_in, 16)
            sp.dma_start(out[TILES], padding[:, 0:D]).then_inc(zero_in, 16)
            sp.wait_ge(taken_out, 1)
            for e in range(E):
                row = sp.value_load(plan_i[0:1, 2, e:e + 1], min_val=0, max_val=SPARE - P)
                sp.dma_start(routed[bass.ds(row, P), :], padding[:]).then_inc(zero_in, 16)
            sp.wait_ge(plan_out, 1)
            sp.wait_ge(routed_out, 32 * TILES)
            sp.wait_ge(zero_in, 16 * (E + 2))

            def load_tile(t):
                if not first(t):
                    sp.wait_ge(xet_done, t)
                    sp.wait_ge(info_kept, t)
                row = sp.value_load(plan_i[0:1, 1, bass.ds(t, 1)], min_val=0, max_val=SPARE)
                sp.dma_start(xe[:], routed[bass.ds(row, P), :]).then_inc(xe_in, 16)

            load_tile(0)
            with sp.Fori(1, MOE_TILES) as t:
                load_tile(t)

        @block.scalar
        def _(act):
            for dst, src in ((ident_sb[:], ident), (head_mask_sb[:], head_mask)):
                act.dma_start(dst, src).then_inc(first_in, 16)
            for dst, src in ((fold_mask_sb[:], fold_mask), (query_eye_sb[:], query_eye),
                             (expert_row_sb[:], expert_row), (token_row_sb[:], token_row),
                             (causal_sb[:], causal), (tri_sb[:], tri), (expand_sb[:], expand),
                             (tile_row_sb[:], tile_row), (bias_qk_sb[:], bias_qk), (wg_sb[:], wg)):
                act.dma_start(dst, src).then_inc(consts_in, 16)

            def round_ctx(t, b):
                n = t * BT + b
                act.wait_ge(ctx_in, 16 * (n + 1))
                if not (isinstance(t, int) and n < 2):
                    act.wait_ge(proj_done, (n - 1) * 3)
                nc.scalar.copy(ctx_hi[:, b % 2], ctx_sb[:]).then_inc(ctx_hi_out, 1)

            def copy_proj(t, b, k):
                n = (t * BT + b) * 3 + k
                bank_of = proj_ps[(b * 3 + k) % 2]
                act.wait_ge(proj_done, n + 1)
                if k < 2:
                    nc.scalar.copy(k_hi[:, b % 2, k], bank_of[:, 0:M_EVEN]).then_inc(proj_out, 1)
                else:
                    nc.scalar.copy(v_sb[:, b % 2], bank_of[:].rearrange("p (m d) -> p m d", m=2))\
                        .then_inc(proj_out, 1)

            def copy_pt(t, u):
                n = t * UNITS + u
                act.wait_ge(pt_done, n + 1)
                if not (isinstance(t, int) and n < 2):
                    act.wait_ge(pv_done, n - 1)
                nc.scalar.copy(prob_t[:, u % 2], pt_ps[:, 0:2 * P].rearrange("p (m n) -> p m n", m=2))\
                    .then_inc(pt_out, 1)

            def copy_xt(t, k, dst, src):
                act.wait_ge(xt_done[k], t + 1)
                nc.scalar.copy(dst[:], src[:, 0:C * P].rearrange("p (c n) -> p c n", c=C)).then_inc(xt_out[k], 1)

            def copy_q(t):
                act.wait_ge(q_done, t + 1)
                if not first(t):
                    act.wait_ge(heads_done, t * BT)
                nc.scalar.copy(q_t[:], f_ps[:, 0:C * P].rearrange("p (c n) -> p c n", c=C))
                nc.scalar.copy(q_hi[:], f_ps[:, 0:C * P].rearrange("p (c n) -> p c n", c=C)).then_inc(q_out, 1)

            def exponentials(t, u):
                b, g = u // G, u % G
                n = t * UNITS + u
                act.wait_ge(max_done, n + 1)
                if not (isinstance(t, int) and n < P_SLOTS):
                    act.wait_ge(pt_done, n - P_SLOTS + 1)
                    if g == 0:
                        act.wait_ge(last_copied, t * BT + b)
                if u == 0 and not first(t):
                    act.wait_ge(sums_inverted, t)
                nc.scalar.activation(prob[:, u % P_SLOTS], score_ps[u % 2][:, 0:M], ACT.Exp,
                                     bias=neg_max[:, u:u + 1], scale=1.0,
                                     accum_out=row_sum[:, g, b:b + 1]).then_inc(exp_done, 1)

            def last_column(t, b):
                act.wait_ge(exp_done, (t * BT + b + 1) * G)
                if b == 0 and not first(t):
                    act.wait_ge(stats_done, t)
                s = (b * G) % P_SLOTS
                apart(act)
                nc.scalar.copy(inv_stat[:, :, 1, b], prob[:, s:s + G, M - 1]).then_inc(last_copied, 1)

            act.wait_ge(setup, 4)
            act.wait_ge(first_in, FIRST)
            nc.scalar.copy(kv_hi[:], kv_raw).then_inc(kv_hi_out, 1)
            round_ctx(0, 0)
            copy_xt(0, 0, xn1_t, f_ps)
            round_ctx(0, 1)
            copy_q(0)
            for k in range(3):
                copy_proj(0, 0, k)
            act.wait_ge(tail_done, 1)
            nc.scalar.copy(v_tail[:], f_ps[:, 0:C * B].rearrange("p (c b) -> p c b", c=C)).then_inc(tail_out, 1)

            def body(i):
                att, nxt, rest, late = phases(i)
                for u in range(UNITS):
                    b, g = u // G, u % G
                    if late and u == 3:
                        act.wait_ge(mt_done, i - 1)
                        nc.scalar.copy(merged_t[:], f_ps[:, 0:C * P].rearrange("p (c n) -> p c n", c=C))\
                            .then_inc(mt_out, 1)
                    if late and u == 6:
                        copy_xt(i - 2, 2, xn3_t, f_ps)
                    if rest and u == 8:
                        copy_xt(i - 1, 1, xn2_t, c_ps)
                    if nxt and u == 11:
                        copy_xt(i + 1, 0, xn1_t, f_ps)
                    if nxt and u == 13:
                        copy_q(i + 1)
                    if att and u >= 2:
                        copy_pt(i, u - 2)
                    if rest and u < 2:
                        copy_pt(i - 1, UNITS - 2 + u)
                    if att:
                        exponentials(i, u)
                    if late and u == 6:
                        nc.scalar.copy(xn3[:, 1, 0:D], xn3[:, 0, 0:D]).then_inc(twin_out, 1)
                    if att and u == 4:
                        act.wait_ge(piece_in, 16 * (i + 1))
                        nc.scalar.copy(expert_hi[:, bass.ds(i * PIECE, PIECE)], piece).then_inc(piece_hi_out, 1)
                    if late and u == 8:
                        act.wait_ge(gap_out, i - 1)
                        apart(act)
                        nc.scalar.activation(exp_gap[:, 0:1], exp_gap[:, 0:1], ACT.Exp).then_inc(gap_exp, 1)
                    if att and g == 3:
                        last_column(i, b)
                    if att and g != 2 and b < 3:
                        copy_proj(i, b + 1, min(g, 2))
                    elif att and g != 2 and nxt:
                        copy_proj(i + 1, 0, min(g, 2))
                    if att and g == 0 and (b < 2 or nxt):
                        round_ctx(i + b // 2, (b + 2) % BT)
                    if rest and u == 9:
                        act.wait_ge(qkb_out, i)
                        nc.scalar.activation(qk_min[:], qk_min[:], ACT.Exp).then_inc(qke_out, 1)
            iterations(act, body)

            def expert_tile(t):
                act.wait_ge(u_done, t + 1)
                if not first(t):
                    act.wait_ge(ht_done, t)
                nc.scalar.activation(hid[:], bank[0][:], ACT.Sigmoid).then_inc(sig_out, 1)

            def copy_hid(t):
                act.wait_ge(ht_done, t + 1)
                if not first(t):
                    act.wait_ge(y_done, t)
                nc.scalar.copy(hid_hi[:], bank[3][:].rearrange("p (c n) -> p c n", c=FC)).then_inc(ht_out, 1)

            def copy_xe(t):
                act.wait_ge(xet_done, t + 1)
                nc.scalar.copy(xe_hi[:], bank[2][:, 0:C * P].rearrange("p (c n) -> p c n", c=C))\
                    .then_inc(xe_hi_out, 1)

            copy_xe(0)
            expert_tile(0)
            copy_xe(1)
            with act.Fori(1, MOE_TILES - 1) as t:
                copy_hid(t - 1)
                expert_tile(t)
                copy_xe(t + 1)
            copy_hid(MOE_TILES - 2)
            expert_tile(MOE_TILES - 1)
            copy_hid(MOE_TILES - 1)

        @block.gpsimd
        def _(pool):
            nc.gpsimd.memset(neg_half[:], -0.5).then_inc(setup, 1)
            nc.gpsimd.memset(padding[:], 0.0).then_inc(setup, 1)
            nc.gpsimd.memset(v_aug[:], 1.0).then_inc(setup, 1)
            nc.gpsimd.memset(ctx_sb[:, :, M:M_EVEN], 0.0).then_inc(setup, 1)
            pool.wait_ge(setup, 4)
            pool.wait_ge(first_in, FIRST)
            nc.gpsimd.tensor_scalar(scaled_mask_sb[:], head_mask_sb[:], float(HD) ** -0.5, None, ALU.mult)\
                .then_inc(setup, 1)
            pool.wait_ge(setup, 5)

            def rstd(t, k):
                pool.wait_ge(ln_var[k], t + 1)
                apart(pool)
                nc.gpsimd.tensor_scalar(ln[k][:, 9:10], ln[k][:, 7:8], LN_EPS, None, ALU.add)\
                    .then_inc(ln_eps_done[k], 1)
                pool.wait_ge(ln_eps_done[k], t + 1)
                nc.gpsimd.tensor_tensor(ln[k][:, 8:9], ln[k][:, 9:10], neg_half[:], ALU.pow)\
                    .then_inc(ln_rstd[k], 1)

            def split_heads(t, b):
                n = t * BT + b
                if b == 0:
                    pool.wait_ge(q_out, t + 1)
                    nc.gpsimd.tensor_tensor(q_lo[:], q_t[:], q_hi[:].bitcast(f32), ALU.subtract)\
                        .then_inc(q_lo_out, 1)
                    pool.wait_ge(q_lo_out, t + 1)
                if not (isinstance(t, int) and n < 2):
                    pool.wait_ge(score_done, (n - 1) * G)
                msk = scaled_mask_sb[:].unsqueeze(1).unsqueeze(3).broadcast_to([P, C, 2 * JH, NQ])
                for heads, q in ((heads_hi, q_hi), (heads_lo, q_lo)):
                    src = q[:, :, b * NQ:(b + 1) * NQ].bitcast(f32).unsqueeze(2).broadcast_to([P, C, 2 * JH, NQ])
                    last = nc.gpsimd.tensor_tensor(heads[:, b % 2], src, msk, ALU.mult)
                last.then_inc(heads_done, 1)

            def ctx_remainder(t, b):
                pool.wait_ge(ctx_hi_out, t * BT + b + 1)
                nc.gpsimd.tensor_tensor(ctx_lo[:, b % 2], ctx_sb[:], ctx_hi[:, b % 2].bitcast(f32),
                                        ALU.subtract).then_inc(ctx_lo_out, 1)

            def load_rest(e):
                pool.dma_start(expert_lo[:, e * W_EXPERT:(e + 1) * W_EXPERT].rearrange("p (k n) -> p k n", k=W_PARTS),
                               w_rest[e * W_PARTS:(e + 1) * W_PARTS].rearrange("k p n -> p k n")).then_inc(rest_in, 16)

            rstd(0, 0)
            ctx_remainder(0, 0)
            split_heads(0, 0)
            ctx_remainder(0, 1)
            pool.wait_ge(consts_in, CONSTS)

            def body(i):
                att, nxt, rest, late = phases(i)
                for u in range(UNITS):
                    b, g = u // G, u % G
                    if isinstance(i, int) and i == TILES and u == 3:
                        pool.wait_ge(piece_stored, 16 * TILES)
                        pool.wait_ge(pv_done, UNITS * TILES)
                        pool.wait_ge(o_step, BT * TILES)
                        for e in range(EARLY):
                            load_rest(e)
                    if isinstance(i, int) and i == TILES + 1 and u == 0:
                        pool.wait_ge(av_done, 2 * TILES)
                        pool.wait_ge(x1b_done, TILES)
                        for e in range(EARLY, MIDDLE):
                            load_rest(e)
                    if rest and u == 0:
                        pool.wait_ge(last_copied, i * BT)
                        pool.wait_ge(sums_inverted, i)
                        if not (isinstance(i, int) and i < 2):
                            pool.wait_ge(ex_done, i - 1)
                        src = inv_stat[:].rearrange("p g w b -> p (g w b)").unsqueeze(2)\
                            .broadcast_to([P, G * 2 * BT, NQ])
                        eye = query_eye_sb[:].unsqueeze(1).broadcast_to([P, G * 2 * BT, NQ])
                        nc.gpsimd.tensor_tensor(stat_rows[:].rearrange("p g w n -> p (g w) n"), src, eye,
                                                ALU.mult).then_inc(stats_done, 1)
                    if att and g == 1 and b < 3:
                        split_heads(i, b + 1)
                    if nxt and u == 15:
                        split_heads(i + 1, 0)
                    if rest and u == 2:
                        pool.wait_ge(xres_in, i * 16)
                        nc.gpsimd.tensor_tensor(x_res[:], x_res[:], bias_sb[:, 0], ALU.add).then_inc(xb_done, 1)
                    if nxt and u == 3:
                        rstd(i + 1, 0)
                    if late and u == 4:
                        rstd(i - 2, 2)
                    if isinstance(i, int) and i == TILES + 1 and u == 4:
                        pool.wait_ge(wo2_done, TILES)
                        load_rest(MIDDLE)
                    if rest and u == 6:
                        rstd(i - 1, 1)
                    if att and u == 7:
                        pool.wait_ge(piece_hi_out, i + 1)
                        nc.gpsimd.tensor_tensor(piece, piece, expert_hi[:, bass.ds(i * PIECE, PIECE)].bitcast(f32),
                                                ALU.subtract).then_inc(piece_lo_out, 1)
                    if rest and u == 10:
                        pool.wait_ge(phi_out, i)
                        if not (isinstance(i, int) and i < 2):
                            pool.wait_ge(sc2_done, (i - 1) * G)
                        split_phi(nc.gpsimd, 1).then_inc(phi1_out, 1)
                    if rest and u == 12:
                        pool.wait_ge(x1_out, i)
                        pool.wait_ge(ln_out[1], i)
                        nc.gpsimd.tensor_tensor(x1[:], x1[:], bias_sb[:, 2], ALU.add).then_inc(x1b_done, 1)
                    if late and u == 12:
                        pool.wait_ge(slot_out, i - 1)
                        pool.wait_ge(twin_out, i - 1)
                        pool.wait_ge(rows_ready, i - 1)
                        for r in range(TOPK):
                            apart(pool)
                            pool.indirect_dma_start(
                                routed, bass.IndirectOffsetOnAxis(ap=slot[:, r:r + 1], axis=0), xn3[:, r], None)\
                                .then_inc(routed_out, 16)
                    if att and g == 1 and (b < 2 or nxt):
                        ctx_remainder(i + b // 2, (b + 2) % BT)
            iterations(pool, body)

            pool.wait_ge(routed_out, 32 * TILES)
            pool.wait_ge(x2_stored, 16 * TILES)
            for e in range(MIDDLE + 1, E):
                load_rest(e)

            def add_tile(t):
                if not first(t):
                    pool.wait_ge(ye_stored, 16 * t)
                pool.wait_ge(info_kept, t + 1)
                apart(pool)
                nc.gpsimd.tensor_copy(to_row[:], row_info[:, bass.ds(t, 1), 0]).then_inc(to_row_out, 1)
                pool.wait_ge(to_row_out, t + 1)
                pool.wait_ge(ye_out, t + 1)
                apart(pool)
                pool.indirect_dma_start(out.rearrange("t p d -> (t p) d"),
                                        bass.IndirectOffsetOnAxis(ap=to_row[:], axis=0), ye[:], None,
                                        compute_op=ALU.add).then_inc(ye_stored, 16)

            pool.wait_ge(x2_stored, 16 * TILES)
            pool.wait_ge(zero_in, 16 * (E + 2))
            add_tile(0)
            with pool.Fori(1, MOE_TILES) as t:
                add_tile(t)
            pool.wait_ge(ye_stored, 16 * MOE_TILES)

        @block.vector
        def _(dve):
            dve.wait_ge(setup, 5)

            def norm_stats(t, k, src):
                nc.vector.bn_stats(ln[k][:, 0:6], src).then_inc(ln_step[k], 1)
                dve.wait_ge(ln_step[k], t + 1)
                apart(dve)
                nc.vector.bn_aggr(ln[k][:, 6:8], ln[k][:, 0:6]).then_inc(ln_var[k], 1)

            def norm_scale(t, k, src, dst):
                dve.wait_ge(ln_rstd[k], t + 1)
                nc.vector.tensor_scalar(dst, src, ln[k][:, 6:7], ln[k][:, 8:9], ALU.subtract, ALU.mult)\
                    .then_inc(ln_out[k], 1)

            def negative_max(t, u):
                dve.wait_ge(score_done, t * UNITS + u + 1)
                nc.vector.tensor_reduce(neg_max[:, u:u + 1], score_ps[u % 2][:, 0:M], AX, ALU.max, negate=True)\
                    .then_inc(max_done, 1)

            def keys_remainder(t, b, k):
                n = (t * BT + b) * 3 + k
                dve.wait_ge(proj_out, n + 1)
                nc.vector.tensor_tensor(k_lo[:, b % 2, k], proj_ps[(b * 3 + k) % 2][:, 0:M_EVEN],
                                        k_hi[:, b % 2, k].bitcast(f32), ALU.subtract).then_inc(k_lo_out, 1)

            def fold_o(t, b):
                n = t * BT + b
                dve.wait_ge(pv_done, (n + 1) * G)
                ps = o_ps[:, 0:C * P].rearrange("p (c j n) -> p c j n", c=C, j=JH)
                msk = fold_mask_sb[:].unsqueeze(1).unsqueeze(3).broadcast_to([P, C, JH, NQ])
                nc.vector.tensor_tensor(o_masked[:], ps, msk, ALU.mult).then_inc(o_out, 1)
                dve.wait_ge(o_out, n + 1)
                nc.vector.tensor_reduce(o_t[:, :, b], o_masked[:].rearrange("p c j n -> p c n j"), AX, ALU.add)\
                    .then_inc(o_step, 1)

            norm_src = x_ln1[:]
            dve.wait_ge(xln_in, 16)
            norm_stats(0, 0, norm_src)
            norm_scale(0, 0, norm_src, xn1[:])
            dve.wait_ge(kv_hi_out, 1)
            nc.vector.tensor_tensor(kv_lo[:], kv_raw, kv_hi[:].bitcast(f32), ALU.subtract).then_inc(kv_lo_out, 1)
            for k in range(2):
                keys_remainder(0, 0, k)
            dve.wait_ge(consts_in, CONSTS)
            nc.vector.tensor_copy(row_next[:], expert_row_sb[:, 1]).then_inc(setup, 1)
            nc.vector.tensor_copy(token_no[:], token_row_sb[:, 0:1]).then_inc(setup, 1)
            nc.vector.tensor_copy(padding[:, D:D + 1], token_row_sb[:, 1:2]).then_inc(setup, 1)

            def merge_heads(t):
                dve.wait_ge(av_done, 2 * (t + 1))
                ps = c_ps[:, 0:H * (HD + 1)].rearrange("p (h d) -> p h d", h=H)
                nc.vector.tensor_scalar(den[:], ps[:, :, HD], ATT_EPS, None, ALU.add).then_inc(av_step, 1)
                dve.wait_ge(av_step, t * 2 + 1)
                nc.vector.reciprocal(den[:], den[:]).then_inc(av_step, 1)
                dve.wait_ge(av_step, t * 2 + 2)
                nc.vector.tensor_tensor(merged[:], ps[:, :, 0:HD],
                                        den[:].unsqueeze(2).broadcast_to([P, H, HD]), ALU.mult)\
                    .then_inc(merged_out, 1)

            def finish_cross(t):
                dve.wait_ge(ex_done, t + 1)
                dve.wait_ge(o_step, (t + 1) * BT)
                ex = c_ps[:].rearrange("p (c w n) -> p c w n", c=C, w=2)
                ext = c_ps[:].rearrange("p (c w b n) -> p c w b n", c=C, w=2, b=BT)
                vt = v_tail[:, :, bass.ds(t * BT, BT)].unsqueeze(3).broadcast_to([P, C, BT, NQ])
                nc.vector.tensor_tensor(o_tail[:].rearrange("p c (b n) -> p c b n", b=BT),
                                        ext[:, :, 1], vt, ALU.mult).then_inc(ex_step, 1)
                dve.wait_ge(ex_step, t * 2 + 1)
                nc.vector.tensor_tensor(o_tail[:], o_tail[:], o_t[:].rearrange("p c b n -> p c (b n)"),
                                        ALU.add).then_inc(ex_step, 1)
                dve.wait_ge(ex_step, t * 2 + 2)
                nc.vector.tensor_tensor(o_tail[:], o_tail[:], ex[:, :, 0], ALU.mult).then_inc(norm_out, 1)

            def add_x2(t):
                dve.wait_ge(wo2_done, t + 1)
                dve.wait_ge(x1b_done, t + 1)
                if not first(t):
                    dve.wait_ge(x2_stored, 16 * t)
                nc.vector.tensor_tensor(x2[:], f_ps[:, 0:D], x1[:], ALU.add).then_inc(x2_out, 1)
                dve.wait_ge(x2_out, t + 1)
                norm_stats(t, 2, x2[:])

            def choose(r):
                dve.wait_ge(lg_done, r + 1)
                nc.vector.tensor_copy(logits[:], f_ps[:, 0:E]).then_inc(lg_step, 1)
                dve.wait_ge(lg_step, r * 5 + 1)
                apart(dve)
                nc.vector.max(top[:], logits[:]).then_inc(lg_step, 1)
                dve.wait_ge(lg_step, r * 5 + 2)
                apart(dve)
                nc.vector.max_index(top_at[:], top[:], logits[:]).then_inc(lg_step, 1)
                nc.vector.tensor_tensor(exp_gap[:, 0:1], top[:, 1:2], top[:, 0:1], ALU.subtract)\
                    .then_inc(gap_out, 1)
                dve.wait_ge(lg_step, r * 5 + 3)
                nc.vector.tensor_copy(top_f[:], top_at[:, 0:TOPK]).then_inc(lg_step, 1)
                dve.wait_ge(lg_step, r * 5 + 4)
                nc.vector.tensor_tensor(chosen[:],
                                        expert_row_sb[:, 0].unsqueeze(1).broadcast_to([P, TOPK, E]),
                                        top_f[:].unsqueeze(2).broadcast_to([P, TOPK, E]), ALU.is_equal)\
                    .then_inc(lg_step, 1)
                dve.wait_ge(lg_step, r * 5 + 5)
                nc.vector.tensor_tensor(chosen_any[:], chosen[:, 0], chosen[:, 1], ALU.add)\
                    .then_inc(any_out, 1)

            def weigh(r):
                dve.wait_ge(gap_exp, r + 1)
                nc.vector.tensor_scalar(exp_gap[:, 1:2], exp_gap[:, 0:1], 1.0, None, ALU.add)\
                    .then_inc(weight_step, 1)
                dve.wait_ge(weight_step, r * 3 + 1)
                nc.vector.reciprocal(pair_weight[:, 0:1], exp_gap[:, 1:2]).then_inc(weight_step, 1)
                nc.vector.tensor_copy(xn3[:, :, D], token_no[:].broadcast_to([P, TOPK])).then_inc(pair_out, 1)
                dve.wait_ge(weight_step, r * 3 + 2)
                nc.vector.tensor_tensor(pair_weight[:, 1:2], pair_weight[:, 0:1], exp_gap[:, 0:1], ALU.mult)\
                    .then_inc(weight_step, 1)
                dve.wait_ge(pair_out, r + 1)
                nc.vector.tensor_scalar(token_no[:], token_no[:], float(P), None, ALU.add)
                dve.wait_ge(weight_step, r * 3 + 3)
                nc.vector.tensor_copy(xn3[:, :, D + 1], pair_weight[:]).then_inc(rows_ready, 1)

            def rank(r):
                dve.wait_ge(rank_done, r + 1)
                nc.vector.tensor_tensor(pos[:], f_ps[:, 0:E], row_next[:], ALU.add).then_inc(rank_step, 1)
                dve.wait_ge(rank_step, r * 4 + 1)
                nc.vector.tensor_tensor(row_next[:], f_ps[:, E:2 * E], row_next[:], ALU.add)\
                    .then_inc(rank_step, 1)
                nc.vector.tensor_tensor(pos_chosen[:], chosen[:],
                                        pos[:].unsqueeze(1).broadcast_to([P, TOPK, E]), ALU.mult)\
                    .then_inc(rank_step, 1)
                dve.wait_ge(rank_step, r * 4 + 3)
                nc.vector.tensor_reduce(slot_f[:], pos_chosen[:], AX, ALU.add).then_inc(rank_step, 1)
                dve.wait_ge(rank_step, r * 4 + 4)
                if not first(r):
                    dve.wait_ge(routed_out, 32 * r)
                nc.vector.tensor_copy(slot[:], slot_f[:]).then_inc(slot_out, 1)

            def biases(t):
                dve.wait_ge(v2_done, t + 1)
                if not first(t):
                    dve.wait_ge(av_done, 2 * t)
                nc.vector.tensor_tensor(v_aug[:, :, 0:HD], f_ps[:, 0:D].rearrange("p (h d) -> p h d", h=H),
                                        bias_sb[:, 1].rearrange("p (h d) -> p h d", h=H), ALU.add)\
                    .then_inc(v2_out, 1)
                dve.wait_ge(qk_done, t + 1)
                bqk = bias_qk_sb[:].unsqueeze(2).broadcast_to([P, 4, P])
                nc.vector.tensor_tensor(qk_phi[:], c_ps[:].rearrange("p (k n) -> p k n", k=4), bqk, ALU.add)\
                    .then_inc(qkb_step, 1)
                dve.wait_ge(qkb_step, t + 1)
                nc.vector.tensor_scalar(qk_min[:], qk_phi[:], 0.0, None, ALU.min).then_inc(qkb_out, 1)

            def mask_scores(t, g):
                dve.wait_ge(sc2_done, t * G + g + 1)
                src = (c_ps, f_ps)[g % 2][:].rearrange("p (j n) -> p j n", j=JH)
                nc.vector.tensor_tensor(a_t[:, g * JH:(g + 1) * JH], src,
                                        causal_sb[:].unsqueeze(1).broadcast_to([P, JH, P]), ALU.mult)\
                    .then_inc(sc2_out, 1)

            def body(i):
                att, nxt, rest, late = phases(i)
                for u in range(UNITS):
                    b, g = u // G, u % G
                    if att:
                        negative_max(i, u)
                    if rest and u == 0:
                        dve.wait_ge(exp_done, i * UNITS)
                        if not (isinstance(i, int) and i < 2):
                            dve.wait_ge(stats_done, i - 1)
                        nc.vector.reciprocal(inv_stat[:, :, 0], row_sum[:]).then_inc(sums_inverted, 1)
                    if att and u >= 3 and (u - 3) % G == 3:
                        fold_o(i, (u - 3) // G)
                    if rest and u == 2:
                        fold_o(i - 1, BT - 1)
                    if late and u == 5:
                        if not (isinstance(i, int) and i < 3):
                            dve.wait_ge(routed_out, 32 * (i - 2))
                        norm_scale(i - 2, 2, x2[:], xn3[:, 0, 0:D])
                    if att and g in (1, 2) and b < 3:
                        keys_remainder(i, b + 1, g - 1)
                    elif att and g in (1, 2) and nxt:
                        keys_remainder(i + 1, 0, g - 1)
                    if late and u == 1:
                        merge_heads(i - 2)
                    if nxt and u == 2:
                        dve.wait_ge(xln_in, 16 * (i + 2))
                        norm_stats(i + 1, 0, x_ln1[:])
                    if rest and u == 4:
                        finish_cross(i - 1)
                    if nxt and u == 5:
                        dve.wait_ge(xt_done[0], i + 1)
                        norm_scale(i + 1, 0, x_ln1[:], xn1[:])
                    if late and u == 7:
                        choose(i - 2)
                    if rest and u == 10:
                        dve.wait_ge(qke_out, i)
                        nc.vector.scalar_tensor_tensor(qk_phi[:], qk_phi[:], 0.0, qk_min[:], ALU.max, ALU.add)\
                            .then_inc(phi_out, 1)
                    if rest and u == 11:
                        dve.wait_ge(piece_stored, 16 * (i if isinstance(i, int) and i >= TILES else i + 1))
                        dve.wait_ge(phi_out, i)
                        if not (isinstance(i, int) and i < 2):
                            dve.wait_ge(sc2_done, (i - 1) * G)
                        split_phi(nc.vector, 0).then_inc(phi0_out, 1)
                    if late and u == 11:
                        weigh(i - 2)
                    if rest and u == 15:
                        mask_scores(i - 1, 3)
                    if late and u == 3:
                        add_x2(i - 2)
                    if rest and u == 5:
                        dve.wait_ge(wo1_done, i)
                        dve.wait_ge(xb_done, i)
                        nc.vector.tensor_tensor(x1[:], c_ps[:, 0:D], x_res[:], ALU.add).then_inc(x1_out, 1)
                        dve.wait_ge(x1_out, i)
                        norm_stats(i - 1, 1, x1[:])
                    if rest and u == 6:
                        norm_scale(i - 1, 1, x1[:], xn2[:])
                    if rest and u == 8:
                        biases(i - 1)
                    if late and u == 9:
                        rank(i - 2)
                    if rest and u in (12, 13, 14):
                        mask_scores(i - 1, u - 12)
            iterations(dve, body)

            n_steps = [0]

            def step(ins):
                n_steps[0] += 1
                ins.then_inc(plan_step, 1)
                dve.wait_ge(plan_step, n_steps[0])

            count, n_tiles, end, skip = (plan[:, k, 0:E] for k in range(4))
            expert_of, row_of, passed = (plan[:, k] for k in range(4, 7))
            base = expert_row_sb[:, 1]
            taken = plan_i[:, 2, 0:E]
            dve.wait_ge(rank_step, 4 * TILES)
            nc.vector.tensor_copy(taken, row_next[:]).then_inc(taken_out, 1)
            step(nc.vector.tensor_tensor(count, row_next[:], base, ALU.subtract))
            step(nc.vector.tensor_scalar(count, count, float(P - 1), None, ALU.add))
            tiles_i = plan_i[:, 0, 0:E]
            step(nc.vector.tensor_copy(tiles_i, count))
            step(nc.vector.tensor_scalar(tiles_i, tiles_i, 7, None, ALU.logical_shift_right))
            step(nc.vector.tensor_copy(n_tiles, tiles_i))
            step(nc.vector.tensor_copy(end[:, 0:1], n_tiles[:, 0:1]))
            for e in range(1, E):
                step(nc.vector.tensor_tensor(end[:, e:e + 1], end[:, e - 1:e], n_tiles[:, e:e + 1], ALU.add))
            step(nc.vector.tensor_scalar(skip, n_tiles, float(-P), float(REGION), ALU.mult, ALU.add))
            step(nc.vector.memset(expert_of, 0.0))
            step(nc.vector.tensor_scalar(row_of, tile_row_sb[:], float(P), None, ALU.mult))
            for e in range(E - 1):
                step(nc.vector.tensor_scalar(passed, tile_row_sb[:], end[:, e:e + 1], None, ALU.is_ge))
                step(nc.vector.tensor_tensor(expert_of, expert_of, passed, ALU.add))
                step(nc.vector.scalar_tensor_tensor(row_of, passed, skip[:, e:e + 1], row_of, ALU.mult, ALU.add))
            step(nc.vector.tensor_scalar(passed, tile_row_sb[:], end[:, E - 1:E], float(SPARE),
                                         ALU.is_ge, ALU.mult))
            step(nc.vector.tensor_tensor(row_of, row_of, passed, ALU.add))
            step(nc.vector.tensor_scalar(row_of, row_of, float(SPARE), None, ALU.min))
            digits = passed
            step(nc.vector.tensor_copy(digits, expert_of))
            step(nc.vector.scalar_tensor_tensor(digits[:, 0:MOE_TILES - 1], expert_of[:, 1:], float(E),
                                                expert_of[:, 0:MOE_TILES - 1], ALU.mult, ALU.add))
            step(nc.vector.scalar_tensor_tensor(digits[:, 1:], expert_of[:, 0:MOE_TILES - 1], float(E * E),
                                                digits[:, 1:], ALU.mult, ALU.add))
            step(nc.vector.tensor_copy(plan_i[:, 0], digits))
            nc.vector.tensor_copy(plan_i[:, 1], row_of).then_inc(plan_out, 1)

            def rows_remainder(t):
                dve.wait_ge(xe_hi_out, t + 1)
                nc.vector.tensor_tensor(xe_lo[:], bank[2][:, 0:C * P].rearrange("p (c n) -> p c n", c=C),
                                        xe_hi[:].bitcast(f32), ALU.subtract).then_inc(xe_lo_out, 1)

            def keep_info(t):
                dve.wait_ge(xe_in, 16 * (t + 1))
                nc.vector.tensor_copy(row_info[:, bass.ds(t, 1)].rearrange("p a k -> p (a k)"), xe[:, D:ROW])\
                    .then_inc(info_kept, 1)

            def hidden_rows_u(t):
                dve.wait_ge(sig_out, t + 1)
                nc.vector.tensor_tensor(hid[:], bank[0][:], hid[:], ALU.mult).then_inc(hid_step, 1)

            def hidden_rows_v(t):
                dve.wait_ge(hid_step, t + 1)
                dve.wait_ge(gv_done, t + 1)
                nc.vector.tensor_tensor(hid[:], bank[1][:], hid[:], ALU.mult).then_inc(hid_out, 1)

            def hidden_remainder(t):
                dve.wait_ge(ht_out, t + 1)
                nc.vector.tensor_tensor(hid_lo[:], bank[3][:].rearrange("p (c n) -> p c n", c=FC),
                                        hid_hi[:].bitcast(f32), ALU.subtract).then_inc(hid_lo_out, 1)

            def copy_y(t):
                dve.wait_ge(y_done, t + 1)
                if not first(t):
                    dve.wait_ge(ye_stored, 16 * t)
                nc.vector.tensor_scalar(ye[:], bank[4][:, 0:D], row_info[:, bass.ds(t, 1), 1], None, ALU.mult)\
                    .then_inc(ye_out, 1)

            keep_info(0)
            rows_remainder(0)
            keep_info(1)
            hidden_rows_u(0)
            rows_remainder(1)
            hidden_rows_v(0)
            with dve.Fori(1, MOE_TILES - 1) as t:
                hidden_remainder(t - 1)
                keep_info(t + 1)
                hidden_rows_u(t)
                rows_remainder(t + 1)
                hidden_rows_v(t)
                copy_y(t - 1)
            hidden_remainder(MOE_TILES - 2)
            hidden_rows_u(MOE_TILES - 1)
            hidden_rows_v(MOE_TILES - 1)
            copy_y(MOE_TILES - 2)
            hidden_remainder(MOE_TILES - 1)
            copy_y(MOE_TILES - 1)

        @block.tensor
        def _(pe):
            mm, tr = nc.tensor.matmul, nc.tensor.transpose
            pe.wait_ge(first_in, FIRST)

            def transposed(dst, src, sem_):
                for c in range(C):
                    last = tr(dst[:, c * P:(c + 1) * P], src[:, c * P:(c + 1) * P], ident_sb[:])
                last.then_inc(sem_, 1)

            def project(t, b, part):
                k = min(part, 2)
                n = (t * BT + b) * 3 + k
                if part == 0:
                    pe.wait_ge(ctx_hi_out, t * BT + b + 1)
                    pe.wait_ge(ctx_lo_out, t * BT + b + 1)
                if part < 3 and not (isinstance(t, int) and n < 2):
                    pe.wait_ge(proj_out, n - 1)
                    if k != 1:
                        pe.wait_ge(k_lo_out, (t * BT + b) * 2 + (0 if k == 0 else 1))
                dst = proj_ps[(b * 3 + k) % 2]
                wkv, ctx = (kv_hi, kv_lo), (ctx_hi[:, b % 2], ctx_lo[:, b % 2])
                steps = [(d, w, x) for w, x in (PASSES[0], PASSES[2], PASSES[1]) for d in range(C)]
                for s, (d, w, x) in enumerate(steps):
                    if part < 2:
                        to, held, moved = dst[:, 0:M_EVEN], wkv[w][:, 0, d, part * P:(part + 1) * P], ctx[x][:, d]
                    else:
                        m = part - 2
                        to, held, moved = (dst[:, m * D:(m + 1) * D], ctx[x][:, d, m * P:(m + 1) * P],
                                           wkv[w][:, 1, d])
                    last = mm(to, held, moved, start=(s == 0), stop=(s == len(steps) - 1))
                if part != 2:
                    last.then_inc(proj_done, 1)

            def scores(t, u):
                b, g = u // G, u % G
                n = t * UNITS + u
                if g == 0:
                    pe.wait_ge(heads_done, t * BT + b + 1)
                    pe.wait_ge(proj_out, (t * BT + b) * 3 + 2)
                    pe.wait_ge(k_lo_out, (t * BT + b + 1) * 2)
                if not (isinstance(t, int) and n < 2):
                    pe.wait_ge(exp_done, n - 1)
                c, half = g // 2, g % 2
                for s, (w, x) in enumerate(PASSES):
                    q = (heads_hi, heads_lo)[w][:, b % 2, c, half * JH:(half + 1) * JH].rearrange("p j n -> p (j n)")
                    last = mm(score_ps[u % 2][:, 0:M_EVEN], q, (k_hi, k_lo)[x][:, b % 2, c],
                              start=(s == 0), stop=(s == len(PASSES) - 1))
                last.then_inc(score_done, 1)

            def transpose_probs(t, u):
                n = t * UNITS + u
                pe.wait_ge(exp_done, n + 1)
                if not (isinstance(t, int) and n < 1):
                    pe.wait_ge(pt_out, n)
                for m in range(2):
                    last = tr(pt_ps[:, m * P:(m + 1) * P], prob[:, u % P_SLOTS, m * P:(m + 1) * P], ident_sb[:])
                last.then_inc(pt_done, 1)

            def values(t, u):
                b, g = u // G, u % G
                n = t * UNITS + u
                pe.wait_ge(pt_out, n + 1)
                if g == 0:
                    pe.wait_ge(proj_out, (t * BT + b) * 3 + 3)
                    if not (isinstance(t, int) and t * BT + b < 1):
                        pe.wait_ge(o_out, t * BT + b)
                c, half = g // 2, g % 2
                for m in range(2):
                    last = mm(o_ps[64 * half:64 * half + 64, c * P:(c + 1) * P],
                              v_sb[:, b % 2, m, g * 64:(g + 1) * 64], prob_t[:, u % 2, m],
                              start=(m == 0), stop=(m == 1))
                last.then_inc(pv_done, 1)

            def query(t):
                pe.wait_ge(xt_out[0], t + 1)
                for c in range(C):
                    for d in range(C):
                        last = mm(f_ps[:, c * P:(c + 1) * P], w_sb[:, WQ1, d, c * P:(c + 1) * P], xn1_t[:, d],
                                  start=(d == 0), stop=(d == C - 1))
                last.then_inc(q_done, 1)

            pe.wait_ge(ln_out[0], 1)
            transposed(f_ps, xn1, xt_done[0])
            query(0)
            def attend(part):
                for h in range(part * H // 2, (part + 1) * H // 2):
                    last = mm(c_ps[:, h * (HD + 1):(h + 1) * (HD + 1)], a_t[:, h], v_aug[:, h],
                              start=True, stop=True)
                last.then_inc(av_done, 1)

            pe.wait_ge(kv_lo_out, 1)
            for part in range(4):
                project(0, 0, part)
            pe.wait_ge(consts_in, CONSTS)
            pe.wait_ge(q_out, 1)
            for c in range(C):
                for d in range(C):
                    last = mm(f_ps[:, c * B:(c + 1) * B], kv_raw[:, 1, d, c * P:(c + 1) * P], tail_sb[:, d],
                              start=(d == 0), stop=(d == C - 1))
            last.then_inc(tail_done, 1)

            def body(i):
                att, nxt, rest, late = phases(i)
                t, r = i - 1, i - 2
                if isinstance(i, int) and i == 1:
                    pe.wait_ge(later_in, 16)
                for u in range(UNITS):
                    b, g = u // G, u % G
                    if att:
                        scores(i, u)
                    if att and u >= 2:
                        transpose_probs(i, u - 2)
                    if rest and u < 2:
                        transpose_probs(t, UNITS - 2 + u)
                    if att and u >= 3:
                        values(i, u - 3)
                    if rest and u < 3:
                        values(t, UNITS - 3 + u)
                    if att:
                        if b < 3:
                            project(i, b + 1, g)
                        elif nxt:
                            project(i + 1, 0, g)
                    if rest and u == 15:
                        pe.wait_ge(sc2_out, t * G + 3)
                        attend(0)
                    if late and u == 0:
                        pe.wait_ge(sc2_out, r * G + 4)
                        attend(1)
                    if late and u == 2:
                        pe.wait_ge(merged_out, r + 1)
                        transposed(f_ps, merged[:].rearrange("p h d -> p (h d)"), mt_done)
                    if late and u == 3:
                        pe.wait_ge(mt_out, r + 1)
                        for c in range(C):
                            last = mm(f_ps[:, 0:D], merged_t[:, c], w_sb[:, WO2, c], start=(c == 0), stop=(c == C - 1))
                        last.then_inc(wo2_done, 1)
                    if rest and u == 3:
                        pe.wait_ge(stats_done, t + 1)
                        for c in range(C):
                            for half in range(2):
                                last = mm(c_ps[64 * half:64 * half + 64, c * 2 * P:(c + 1) * 2 * P], expand_sb[:],
                                          stat_rows[:, 2 * c + half].rearrange("p w n -> p (w n)"),
                                          start=True, stop=True)
                        last.then_inc(ex_done, 1)
                    if late and u == 5:
                        pe.wait_ge(ln_out[2], r + 1)
                        transposed(f_ps, xn3[:, 0], xt_done[2])
                    if rest and u == 5:
                        pe.wait_ge(norm_out, t + 1)
                        for c in range(C):
                            last = mm(c_ps[:, 0:D], o_tail[:, c], w_sb[:, WO1, c], start=(c == 0), stop=(c == C - 1))
                        last.then_inc(wo1_done, 1)
                    if late and u == 6:
                        pe.wait_ge(xt_out[2], r + 1)
                        for d in range(C):
                            last = mm(f_ps[:, 0:E], xn3_t[:, d], wg_sb[:, d], start=(d == 0), stop=(d == C - 1))
                        last.then_inc(lg_done, 1)
                    if rest and u == 7:
                        pe.wait_ge(ln_out[1], t + 1)
                        transposed(c_ps, xn2, xt_done[1])
                    if rest and u == 8:
                        pe.wait_ge(xt_out[1], t + 1)
                        for k in range(4):
                            w, c = (WQ2, WK2)[k // C], k % C
                            for d in range(C):
                                last = mm(c_ps[:, k * P:(k + 1) * P], w_sb[:, w, d, c * P:(c + 1) * P], xn2_t[:, d],
                                          start=(d == 0), stop=(d == C - 1))
                        last.then_inc(qk_done, 1)
                        if late:
                            pe.wait_ge(lg_step, 5 * r + 1)
                        for d in range(C):
                            last = mm(f_ps[:, 0:D], xn2_t[:, d], w_sb[:, WV2, d], start=(d == 0), stop=(d == C - 1))
                        last.then_inc(v2_done, 1)
                    if late and u == 9:
                        pe.wait_ge(any_out, r + 1)
                        if rest:
                            pe.wait_ge(v2_out, t + 1)
                        for k in range(2):
                            last = mm(f_ps[:, k * E:(k + 1) * E], tri_sb[:, k], chosen_any[:], start=True, stop=True)
                        last.then_inc(rank_done, 1)
                    if nxt and u == 10:
                        pe.wait_ge(ln_out[0], i + 2)
                        if isinstance(i, int) and i == 0:
                            pe.wait_ge(tail_out, 1)
                        if rest:
                            pe.wait_ge(v2_out, t + 1)
                        if late:
                            pe.wait_ge(rank_step, 4 * r + 2)
                        transposed(f_ps, xn1, xt_done[0])
                    if rest and u in (12, 13, 14):
                        for g2 in ((0,), (1,), (2, 3))[u - 12]:
                            if g2 % 2 == 0:
                                pe.wait_ge((phi0_out, phi1_out)[g2 // 2], t + 1)
                            if g2 == 0:
                                pe.wait_ge(v2_out, t + 1)
                            if g2 >= 2:
                                pe.wait_ge(sc2_out, t * G + g2 - 1)
                            if g2 == 1 and nxt:
                                pe.wait_ge(q_out, i + 2)
                            if g2 == 1 and late and not nxt:
                                pe.wait_ge(rank_step, 4 * r + 2)
                            c, half = g2 // 2, g2 % 2
                            mm((c_ps, f_ps)[g2 % 2][:], qk_phi[:, C + c],
                               phi_heads[:, c, half * JH:(half + 1) * JH].rearrange("p j n -> p (j n)"),
                               start=True, stop=True).then_inc(sc2_done, 1)
                    if nxt and u == 12:
                        query(i + 1)
            iterations(pe, body)

            pe.wait_ge(piece_hi_out, TILES)
            pe.wait_ge(rest_in, 16 * E)
            pe.wait_ge(plan_out, 1)

            def transpose_x(t):
                pe.wait_ge(xe_in, 16 * (t + 1))
                transposed(bank[2], xe, xet_done)

            def experts_of(t):
                digits = pe.value_load(plan_i[0:1, 0, bass.ds(t, 1)], min_val=0, max_val=E ** 3 - 1)
                return [pe.snap((digits // E ** k) % E, min_val=0, max_val=E - 1) for k in range(3)]

            def up_part(t, e, k):
                dst, done, read = ((bank[0], u_done, hid_step), (bank[1], gv_done, hid_out))[k]
                weights = expert_weights(k, e)
                pe.wait_ge(xe_hi_out, t + 1)
                if not first(t):
                    pe.wait_ge(read, t)
                steps = [(d, x, w) for x, w in PASSES for d in range(C)]
                for s, (d, x, w) in enumerate(steps):
                    if x == LO and d == 0:
                        pe.wait_ge(xe_lo_out, t + 1)
                    last = mm(dst[:], (xe_hi, xe_lo)[x][:, d], weights[w][:, d],
                              start=(s == 0), stop=(s == len(steps) - 1))
                last.then_inc(done, 1)

            def transpose_h(t):
                pe.wait_ge(hid_out, t + 1)
                for c in range(FC):
                    last = tr(bank[3][:, c * P:(c + 1) * P], hid[:, c * P:(c + 1) * P], ident_sb[:])
                last.then_inc(ht_done, 1)

            def down(t, e):
                weights = expert_weights(2, e)
                pe.wait_ge(ht_out, t + 1)
                if not first(t):
                    pe.wait_ge(ye_out, t)
                steps = [(c, x, w) for x, w in PASSES for c in range(FC)]
                for s, (c, x, w) in enumerate(steps):
                    if x == LO and c == 0:
                        pe.wait_ge(hid_lo_out, t + 1)
                    last = mm(bank[4][:, 0:D], (hid_hi, hid_lo)[x][:, c], weights[w][:, c],
                              start=(s == 0), stop=(s == len(steps) - 1))
                last.then_inc(y_done, 1)

            transpose_x(0)
            e, e_after, _ = experts_of(0)
            up_part(0, e, 0)
            up_part(0, e, 1)
            transpose_x(1)
            up_part(1, e_after, 0)
            with pe.Fori(1, MOE_TILES - 1) as t:
                e, e_after, e_before = experts_of(t)
                transpose_h(t - 1)
                up_part(t, e, 1)
                transpose_x(t + 1)
                down(t - 1, e_before)
                up_part(t + 1, e_after, 0)
            last = MOE_TILES - 1
            e, _, e_before = experts_of(last)
            transpose_h(last - 1)
            up_part(last, e, 1)
            down(last - 1, e_before)
            transpose_h(last)
            down(last, e)


def kernel(x, ctx_1024, L0_xattn_wq, L0_xattn_wk, L0_xattn_wv, L0_xattn_wo, L0_xattn_bo, L0_attn_mask,
           L0_attn_Wq, L0_attn_bq, L0_attn_Wk, L0_attn_bk, L0_attn_Wv, L0_attn_bv, L0_attn_Wo, L0_attn_bo,
           L0_ffn_Wg, L0_ffn_W1, L0_ffn_W2, L0_ffn_W3):
    import numpy as np
    import concourse.bacc as bacc
    from concourse.bass_utils import run_bass_kernel_spmd as run

    def lay(a):
        return np.ascontiguousarray(a)

    def stacked(*ws):
        return lay(np.stack([np.asarray(w).T.reshape(C, P, D).transpose(1, 0, 2) for w in ws], axis=1))

    ctx = np.asarray(ctx_1024)
    rows = np.arange(P)
    head_of = (rows % 64) // HD
    half_of = rows // 64
    arrays = {
        "x": lay(np.asarray(x).reshape(TILES, P, D)),
        "ctx_t": lay(ctx.reshape(TILES, BT, M, C, P).transpose(0, 1, 4, 3, 2)),
        "tail_t": lay(ctx[:, M - 1].reshape(B, C, P).transpose(2, 1, 0)),
        "w_attn": stacked(L0_xattn_wq, L0_xattn_wo, L0_attn_Wq, L0_attn_Wk, L0_attn_Wv, L0_attn_Wo),
        "w_kv": stacked(L0_xattn_wk, L0_xattn_wv),
        "bias_rows": lay(np.stack([np.asarray(v) for v in (L0_xattn_bo, L0_attn_bv, L0_attn_bo)]).reshape(1, 3 * D)),
        "bias_qk": lay(np.stack([np.asarray(L0_attn_bq).reshape(C, P), np.asarray(L0_attn_bk).reshape(C, P)])
                       .reshape(2 * C, P).T),
        "wg": lay(np.asarray(L0_ffn_Wg).reshape(C, P, E).transpose(1, 0, 2)),
        "w_expert": lay(np.concatenate([np.asarray(w).reshape(E, n, P, -1).transpose(0, 2, 1, 3).reshape(E, P, C * F)
                                        for w, n in ((L0_ffn_W1, C), (L0_ffn_W2, C), (L0_ffn_W3, FC))], axis=2)
                        .reshape(E, P, W_PARTS, PIECE).transpose(0, 2, 1, 3).reshape(TILES, P, PIECE)),
        "ident": np.eye(P, dtype=np.float32),
        "head_mask": lay((half_of[:, None] * JH + head_of[:, None] == np.arange(2 * JH)[None]).astype(np.float32)),
        "fold_mask": lay((head_of[:, None] == np.arange(JH)[None]).astype(np.float32)),
        "causal": lay(((rows[:, None] // NQ == rows[None] // NQ) & (rows[:, None] <= rows[None])).astype(np.float32)),
        "tri": lay(np.stack([rows[:, None] < rows[None], rows[:, None] >= 0 * rows[None]], axis=1).astype(np.float32)),
        "expand": lay((rows[:, None] // NQ == head_of[None, 0:64]).astype(np.float32)),
        "query_eye": lay((rows[:, None] % NQ == np.arange(NQ)[None]).astype(np.float32)),
        "expert_row": lay(np.broadcast_to(np.stack([np.arange(E), np.arange(E) * REGION])[None],
                                          (P, 2, E)).astype(np.float32)),
        "token_row": lay(np.stack([rows, TOK + rows], axis=1).astype(np.float32)),
        "tile_row": lay(np.broadcast_to(np.arange(MOE_TILES, dtype=np.float32)[None], (P, MOE_TILES))),
    }
    nc = bacc.Bacc("TRN2", target_bir_lowering=False, num_devices=1)
    aps = {k: nc.dram_tensor(k, v.shape, mybir.dt.from_np(v.dtype), kind="ExternalInput").ap()
           for k, v in arrays.items()}
    f32 = mybir.dt.float32
    routed = nc.dram_tensor("routed", (SPARE + P, ROW), f32, kind="Internal").ap()
    w_rest = nc.dram_tensor("w_rest", (TILES, P, PIECE), f32, kind="Internal").ap()
    out = nc.dram_tensor("out", (TILES + 1, P, D), f32, kind="ExternalOutput").ap()
    perceiver(nc, **aps, routed=routed, w_rest=w_rest, out=out)
    got = run(nc, [arrays], core_ids=[0])
    return got.results[0]["out"][:TILES].reshape(B, NQ, D)
```
